# Optimizing a Trainium2 kernel written in Bass

```python
import numpy as np
import jax
import jax.numpy as jnp

def _softmax(x, axis=-1):
    return jax.nn.softmax(x, axis=axis)

def _gelu(x):
    return jax.nn.gelu(x, approximate=True)

def _silu(x):
    return jax.nn.silu(x)

def _sigmoid(x):
    return jax.nn.sigmoid(x)

def _layernorm(x, axis=-1, eps=1e-05):
    m = jnp.mean(x, axis=axis, keepdims=True)
    v = jnp.var(x, axis=axis, keepdims=True)
    return (x - m) / jnp.sqrt(v + eps)

def _scatter_add(tgt, idx, src, axis=0):
    return tgt.at[idx].add(src)

def _segment_sum(src, seg, n):
    return jax.ops.segment_sum(src, seg, n)
kernel_name = 'mk_flamingo_gated_d1_seqx_r8_f286f3'

def setup_inputs(seed: int=0):
    np.random.seed(seed)
    _w = jnp.asarray

    def _rec_inputs():
        import jax
        import jax.numpy as jnp
        _rk = jax.random.key(seed)
        x = -0.0002928 + 1 * jax.random.normal(jax.random.fold_in(_rk, 1), (2, 512, 128), jnp.float32)
        _lenS = 512 - jax.random.randint(jax.random.fold_in(_rk, 7), (2,), 0, max(1, 512 // 4) + 1, jnp.int32)
        _lenS2 = 32 - jax.random.randint(jax.random.fold_in(_rk, 8), (2,), 0, max(1, 32 // 4) + 1, jnp.int32)
        _ctx_1024P = jax.random.normal(jax.random.fold_in(_rk, 11), (2, 16, 128), jnp.float32)
        _ctx_1024c = jax.random.dirichlet(jax.random.fold_in(_rk, 511), 0.3 * jnp.ones((16,), jnp.float32), (2, 32))
        _ctx_1024t = jnp.einsum('bsk,bkd->bsd', _ctx_1024c, _ctx_1024P)
        _ctx_1024t = _ctx_1024t * jax.lax.rsqrt(jnp.mean(jnp.square(_ctx_1024t)) + 1e-12) * 0.953939
        ctx_1024 = -1.39393e-06 + 0.999914 * (_ctx_1024t + 0.3 * jax.random.normal(jax.random.fold_in(_rk, 611), (2, 32, 128), jnp.float32))
        _g = jax.random.normal(jax.random.fold_in(_rk, 9001), (2, 1), jnp.float32)
        _g = jnp.sign(_g) * jnp.maximum(jnp.abs(_g), 1.0) + (_g == 0) * 1.0
        g_xattn = _g[0]
        g_ffn = _g[1]
        return (x, ctx_1024, g_xattn, g_ffn)
    x, ctx_1024, g_xattn, g_ffn = _rec_inputs()

    def _L0_xattn_setup():
        import jax, jax.numpy as jnp
        import numpy as np
        HEADS = 8
        DIM_HEAD = 64
        DIM = 128
        CTX_DIM = 128
        HIDDEN = HEADS * DIM_HEAD
        key = jax.random.key(seed)
        ks = jax.random.split(key, 7)
        b, n, m = (2, 256, 256)
        x = jax.random.normal(ks[0], (b, n, DIM), dtype=jnp.float32)
        context = jax.random.normal(ks[1], (b, m, CTX_DIM), dtype=jnp.float32)
        Wq = jax.random.normal(ks[2], (DIM, HIDDEN), dtype=jnp.float32) * (1.0 / np.sqrt(DIM))
        Wk = jax.random.normal(ks[3], (CTX_DIM, HIDDEN), dtype=jnp.float32) * (1.0 / np.sqrt(CTX_DIM))
        Wv = jax.random.normal(ks[4], (CTX_DIM, HIDDEN), dtype=jnp.float32) * (1.0 / np.sqrt(CTX_DIM))
        Wo = jax.random.normal(ks[5], (HIDDEN, DIM), dtype=jnp.float32) * (1.0 / np.sqrt(HIDDEN))
        bo = jax.random.normal(ks[6], (DIM,), dtype=jnp.float32) * 0.01
        return {'x': x, 'context': context, 'Wq': Wq, 'Wk': Wk, 'Wv': Wv, 'Wo': Wo, 'bo': bo}
    _L0_xattn_all = _L0_xattn_setup()
    _L0_xattn_in = {k: v for k, v in _L0_xattn_all.items() if k in ('Wq', 'Wk', 'Wv', 'Wo', 'bo')}
    del _L0_xattn_all

    def _L0_ffn_setup():
        import jax, jax.numpy as jnp
        import numpy as np
        TOP_K = 2
        key = jax.random.key(seed)
        k0, k1, k2, k3, k4 = jax.random.split(key, 5)
        B, S, D, H, E = (4, 256, 128, 256, 8)
        x = jax.random.normal(k0, (B, S, D), dtype=jnp.float32)
        router_w = jax.random.normal(k1, (E, D), dtype=jnp.float32) * D ** (-0.5)
        w_gate = jax.random.normal(k2, (E, D, H), dtype=jnp.float32) * D ** (-0.5)
        w_up = jax.random.normal(k3, (E, D, H), dtype=jnp.float32) * D ** (-0.5)
        w_down = jax.random.normal(k4, (E, H, D), dtype=jnp.float32) * H ** (-0.5)
        return {'x': x, 'router_w': router_w, 'w_gate': w_gate, 'w_up': w_up, 'w_down': w_down}
    _L0_ffn_all = _L0_ffn_setup()
    _L0_ffn_in = {k: v for k, v in _L0_ffn_all.items() if k in ('router_w', 'w_gate', 'w_up', 'w_down')}
    del _L0_ffn_all
    return {'x': x, 'ctx_1024': ctx_1024, 'g_xattn': g_xattn, 'g_ffn': g_ffn, 'L0_xattn_Wq': _L0_xattn_in['Wq'], 'L0_xattn_Wk': _L0_xattn_in['Wk'], 'L0_xattn_Wv': _L0_xattn_in['Wv'], 'L0_xattn_Wo': _L0_xattn_in['Wo'], 'L0_xattn_bo': _L0_xattn_in['bo'], 'L0_ffn_router_w': _L0_ffn_in['router_w'], 'L0_ffn_w_gate': _L0_ffn_in['w_gate'], 'L0_ffn_w_up': _L0_ffn_in['w_up'], 'L0_ffn_w_down': _L0_ffn_in['w_down']}

def reference(x, ctx_1024, g_xattn, g_ffn, L0_xattn_Wq, L0_xattn_Wk, L0_xattn_Wv, L0_xattn_Wo, L0_xattn_bo, L0_ffn_router_w, L0_ffn_w_gate, L0_ffn_w_up, L0_ffn_w_down):
    import jax
    import jax.numpy as jnp

    def _L0_xattn_ref(x, context, Wq, Wk, Wv, Wo, bo):
        import jax, jax.numpy as jnp
        import numpy as np
        HEADS = 8
        DIM_HEAD = 64
        DIM = 128
        CTX_DIM = 128
        HIDDEN = HEADS * DIM_HEAD
        b, n, _ = x.shape
        m = context.shape[1]
        scale = DIM_HEAD ** (-0.5)
        q = (x @ Wq).reshape(b, n, HEADS, DIM_HEAD).transpose(0, 2, 1, 3)
        k = (context @ Wk).reshape(b, m, HEADS, DIM_HEAD).transpose(0, 2, 1, 3)
        v = (context @ Wv).reshape(b, m, HEADS, DIM_HEAD).transpose(0, 2, 1, 3)
        scores = jnp.einsum('bhnd,bhmd->bhnm', q, k) * scale
        attn = jax.nn.softmax(scores, axis=-1)
        out = jnp.einsum('bhnm,bhmd->bhnd', attn, v)
        out = out.transpose(0, 2, 1, 3).reshape(b, n, HIDDEN)
        return out @ Wo + bo

    def _L0_ffn_ref(x, router_w, w_gate, w_up, w_down):
        import jax, jax.numpy as jnp
        import numpy as np
        TOP_K = 2
        B, S, D = x.shape
        E = router_w.shape[0]
        xt = x.reshape(-1, D)
        logits = xt @ router_w.T
        topk_vals, topk_idx = jax.lax.top_k(logits, TOP_K)
        g = jax.nn.sigmoid(topk_vals)
        g = g / (g.sum(axis=-1, keepdims=True) + 1e-10)
        out = jnp.zeros_like(xt)
        for e in range(E):
            ge = jnp.sum(jnp.where(topk_idx == e, g, jnp.zeros_like(g)), axis=-1)
            h = jax.nn.silu(xt @ w_gate[e]) * (xt @ w_up[e])
            out = out + ge[:, None] * (h @ w_down[e])
        return out.reshape(B, S, D)
    x = x + jnp.tanh(g_xattn[0]) * _L0_xattn_ref(_layernorm(x, axis=-1), ctx_1024, L0_xattn_Wq, L0_xattn_Wk, L0_xattn_Wv, L0_xattn_Wo, L0_xattn_bo)
    x = x + jnp.tanh(g_ffn[0]) * _L0_ffn_ref(_layernorm(x, axis=-1), L0_ffn_router_w, L0_ffn_w_gate, L0_ffn_w_up, L0_ffn_w_down)
    return x

_drawn_inputs = setup_inputs


def setup_inputs(seed=0):
    import zlib

    import numpy as np

    out = dict(_drawn_inputs(seed))
    spreads = {}
    factors = {}
    for name, (base, spread) in spreads.items():
        noise = np.random.default_rng([zlib.crc32(name.encode()), seed]).standard_normal(out[name].shape)
        drawn = base * np.exp(spread * noise) if base else spread * noise
        out[name] = jnp.asarray(drawn.astype(out[name].dtype))
    for name, factor in factors.items():
        out[name] = (out[name] * factor).astype(out[name].dtype)
    return out
```

```python
from contextlib import ExitStack

import concourse.bass as bass
from concourse import mybir

P = 128
F32 = mybir.dt.float32
F32R = mybir.dt.float32r
U32 = mybir.dt.uint32
ALU = mybir.AluOpType
ACT = mybir.ActivationFunctionType
AX_X = mybir.AxisListType.X


def gated_cross_attention_and_top2_experts(
    nc: bass.Bass,
    x: bass.AP,
    ctx: bass.AP,
    g_xattn: bass.AP,
    g_ffn: bass.AP,
    Wq: bass.AP,
    Wk: bass.AP,
    Wv: bass.AP,
    Wo: bass.AP,
    bo: bass.AP,
    router_w: bass.AP,
    w_gate: bass.AP,
    w_up: bass.AP,
    w_down: bass.AP,
    out: bass.AP,
):
    B, S, D = x.shape
    M = ctx.shape[1]
    HID = Wq.shape[1]
    DH = 64
    HEADS = HID // DH
    E, _, H = w_gate.shape
    T = S // P
    NT = B * T
    HC = HID // P
    HM = HEADS * M
    FC = H // P
    SCALE = DH ** -0.5
    LN_EPS = 1e-5
    GATE_EPS = 1e-10
    assert D == P and B == 2 and S == 512 and HM == 256 and E == 8 and FC == 2

    EP = 2
    ROUNDS = E // EP
    UNITS = EP * B * FC
    PAIRS = EP * B
    LAG = 2
    HEADSTART = 6

    x_rows = x.rearrange("b (p t) d -> p b t d", t=T)
    out_rows = out.rearrange("b (p t) d -> p b t d", t=T)
    ctx_rows = ctx.rearrange("b m d -> (b m) d")
    Wo_rows = Wo.rearrange("(c k) n -> k c n", k=P)

    with ExitStack() as stack:
        def sb(name, shape, dt=F32):
            return stack.enter_context(nc.sbuf_tensor(name, shape, dt))

        def sem(name):
            return stack.enter_context(nc.semaphore(name))

        bank = [stack.enter_context(nc.psum_tensor(f"bank{i}", [P, 512], F32)) for i in range(8)]
        gates_dram = nc.dram_tensor("gates_dram", [E, B * S], F32, kind="Internal").ap()

        ident = sb("ident", [P, P])
        center = sb("center", [P, P])
        expert_no = sb("expert_no", [P, E])
        minus_half = sb("minus_half", [P, T])
        x_sb = sb("x_sb", [P, B, T, D])
        ctx_sb = sb("ctx_sb", [B * M, D])
        wq_sb = sb("wq_sb", [P, HID])
        wk_sb = sb("wk_sb", [P, HID])
        wv_sb = sb("wv_sb", [P, HID])
        wo_sb = sb("wo_sb", [P, HC, D])
        bo_sb = sb("bo_sb", [P, D])
        rw_sb = sb("rw_sb", [E, D])
        g_raw = sb("g_raw", [P, 2])
        g_tanh = sb("g_tanh", [P, 2])
        ctxT = sb("ctxT", [P, B * M])
        rwT = sb("rwT", [P, E])
        rwT_hi = sb("rwT_hi", [P, E], F32R)
        rwT_lo = sb("rwT_lo", [P, E], F32R)
        wqT = sb("wqT", [P, HC, D])
        k_diag = sb("k_diag", [P, HC, 2, B * M])
        v_diag = sb("v_diag", [P, B, 2, 2, P])
        m_sb = sb("m_sb", [P, B, HEADS, M])
        u_sb = sb("u_sb", [P, B, 2, D])
        xT = sb("xT", [P, NT, P])
        stats = sb("stats", [P, NT, 6])
        mean_var = sb("mean_var", [P, NT, 2])
        var_eps = sb("var_eps", [P, B, T])
        rstd = sb("rstd", [P, B, T])
        rstd_scale = sb("rstd_scale", [P, NT])
        x_bias = sb("x_bias", [P, B, T, D])
        row_max = sb("row_max", [P, 2, 2 * HEADS])
        shifted = sb("shifted", [P, 2, 2, HM])
        expd = sb("expd", [P, 2, 2, HM])
        row_sum = sb("row_sum", [P, 2, 2 * HEADS])
        row_inv = sb("row_inv", [P, 2, 2 * HEADS])
        probs = sb("probs", [P, 2, 2, HM])
        probsT = sb("probsT", [P, 2, 2, 2, P])
        x2 = sb("x2", [P, B, T, D])
        stats2 = sb("stats2", [P, NT, 6])
        mean_var2 = sb("mean_var2", [P, NT, 2])
        var_eps2 = sb("var_eps2", [P, B, T])
        rstd2 = sb("rstd2", [P, B, T])
        xn2 = sb("xn2", [P, NT, D])
        xn2T_hi = sb("xn2T_hi", [P, B, S], F32R)
        xn2T_lo = sb("xn2T_lo", [P, B, S], F32R)
        logits = sb("logits", [P, NT, E])
        top8 = sb("top8", [P, NT, 8])
        top8_at = sb("top8_at", [P, NT, 8], U32)
        top2_at = sb("top2_at", [P, B, 2 * T])
        top2_exp = sb("top2_exp", [P, B, 2 * T])
        top2_sig = sb("top2_sig", [P, B, 3, 2 * T])
        gate_sum = sb("gate_sum", [P, B, 2, T])
        is_chosen = sb("is_chosen", [P, B, 2 * T, E])
        gates = sb("gates", [P, NT, E])
        gatesT = sb("gatesT", [E, B * S])
        raw_gu = sb("raw_gu", [P, EP, 2, H])
        raw_d = sb("raw_d", [P, EP, FC, D])
        gu_hi = sb("gu_hi", [P, EP, 2, H], F32R)
        gu_lo = sb("gu_lo", [P, EP, 2, H], F32R)
        d_hi = sb("d_hi", [P, EP, FC, D], F32R)
        d_lo = sb("d_lo", [P, EP, FC, D], F32R)
        silu_g = sb("silu_g", [P, 2, S])
        hid = sb("hid", [P, 2, S])
        hid_hi = sb("hid_hi", [P, 4, S], F32R)
        hid_lo = sb("hid_lo", [P, 4, S], F32R)
        gate_row = sb("gate_row", [P, PAIRS, S])
        weighted = sb("weighted", [P, 2, S])
        acc = sb("acc", [P, B, S])
        y = sb("y", [P, B, T, D])

        in_x = [sem(f"in_x{b}") for b in range(B)]
        in_ctx, in_wq, in_wk, in_wv, in_wo = (sem(f"in_{n}") for n in ("ctx", "wq", "wk", "wv", "wo"))
        in_bo, in_rw, in_g = sem("in_bo"), sem("in_rw"), sem("in_g")
        in_gu = [sem(f"in_gu{i}") for i in range(EP)]
        in_d = [sem(f"in_d{i}") for i in range(EP)]
        in_gate_row = [sem(f"in_gate_row{i}") for i in range(PAIRS)]
        gates_stored = [sem(f"gates_stored{b}") for b in range(B)]
        out_stored = [sem(f"out_stored{b}") for b in range(B)]
        const_made = sem("const_made")
        zeroed = sem("zeroed")
        small_T = sem("small_T")
        small_out = sem("small_out")
        wqT_made, wqT_out = sem("wqT_made"), sem("wqT_out")
        kv_made, k_out, v_out = sem("kv_made"), sem("k_out"), sem("v_out")
        m_made, m_out, u_made, u_out = sem("m_made"), sem("m_out"), sem("u_made"), sem("u_out")
        rw_split = sem("rw_split")
        xT_made, xT_out = sem("xT_made"), sem("xT_out")
        tanh_made = sem("tanh_made")
        bias_made = sem("bias_made")
        ln1 = sem("ln1")
        pow1 = sem("pow1")
        scores_made, shift_made, exp_made = sem("scores_made"), sem("shift_made"), sem("exp_made")
        max_made, stat2_step, gate_step = sem("max_made"), sem("stat2_step"), sem("gate_step")
        sum_made, inv_made, probs_made = sem("sum_made"), sem("inv_made"), sem("probs_made")
        probsT_made, probsT_out = sem("probsT_made"), sem("probsT_out")
        attn_made, x2_made = sem("attn_made"), sem("x2_made")
        ln2, pow2, xn2_made = sem("ln2"), sem("pow2"), sem("xn2_made")
        xn2T_made, xn2_hi_made, xn2_lo_made = sem("xn2T_made"), sem("xn2_hi_made"), sem("xn2_lo_made")
        logits_made, route = sem("logits_made"), sem("route")
        top2_exp_made = sem("top2_exp_made")
        gatesT_made, gatesT_out = sem("gatesT_made"), sem("gatesT_out")
        w_hi_done, w_lo_done = sem("w_hi_done"), sem("w_lo_done")
        gate_done, up_done, down_done = sem("gate_done"), sem("up_done"), sem("down_done")
        silu_done, hid_done, hid_hi_done, hid_lo_done = (
            sem("silu_done"), sem("hid_done"), sem("hid_hi_done"), sem("hid_lo_done"))
        weighted_done, acc_done = sem("weighted_done"), sem("acc_done")
        accT_made, y_made = sem("accT_made"), sem("y_made")

        gate_bank, up_bank, down_bank = bank[0:2], bank[2:4], bank[4:6]

        def unit_of(n):
            m = n % UNITS
            return m // (EP * FC), (m // FC) % EP, m % FC

        block = stack.enter_context(nc.Block())

        @block.sync
        def _(sp):
            sp.dma_start(ctx_sb[:], ctx_rows).then_inc(in_ctx, 16)
            sp.dma_start(wk_sb[:], Wk).then_inc(in_wk, 16)
            sp.dma_start(x_sb[:, 0], x_rows[:, 0]).then_inc(in_x[0], 16)
            sp.dma_start(wv_sb[:], Wv).then_inc(in_wv, 16)
            sp.dma_start(x_sb[:, 1], x_rows[:, 1]).then_inc(in_x[1], 16)

            def load_gate_up(e, k):
                sp.dma_start(raw_gu[:, k, 0], w_gate[e].squeeze(0) if len(w_gate[e].shape) == 3 else w_gate[e]
                             ).then_inc(in_gu[k], 16)
                sp.dma_start(raw_gu[:, k, 1], w_up[e].squeeze(0) if len(w_up[e].shape) == 3 else w_up[e]
                             ).then_inc(in_gu[k], 16)

            def load_down(e, k):
                sp.dma_start(raw_d[:, k], w_down[e].rearrange("(c p) d -> p c d", p=P)).then_inc(in_d[k], 16)

            for k in range(EP):
                load_gate_up(k, k)
                load_down(k, k)

            def load_gate_row(e, q):
                half, k = q // EP, q % EP
                src = gates_dram[bass.ds(e, 1), half * S:(half + 1) * S]
                sp.dma_start(gate_row[:, q], src.broadcast_to([P, S])).then_inc(in_gate_row[q], 16)

            for b in range(B):
                sp.wait_ge(gatesT_out, b + 1)
                sp.dma_start(gates_dram[:, b * S:(b + 1) * S], gatesT[:, b * S:(b + 1) * S]
                             ).then_inc(gates_stored[b], 16)
                sp.wait_ge(gates_stored[b], 16)
                for k in range(EP):
                    load_gate_row(k, b * EP + k)
            with sp.Fori(0, ROUNDS - 1) as j:
                for k in range(EP):
                    sp.wait_ge(w_lo_done, j * 4 + (k + 1))
                    load_gate_up(j * EP + (EP + k), k)
                for k in range(EP):
                    sp.wait_ge(w_lo_done, j * 4 + (k + 3))
                    load_down(j * EP + (EP + k), k)
                for q in range(PAIRS):
                    sp.wait_ge(weighted_done, j * PAIRS + (q + 1))
                    load_gate_row(j * EP + (EP + q % EP), q)
            for b in range(B):
                sp.wait_ge(y_made, b + 1)
                sp.dma_start(out_rows[:, b], y[:, b]).then_inc(out_stored[b], 16)
            for b in range(B):
                sp.wait_ge(out_stored[b], 16)

        @block.gpsimd
        def _(pool):
            nc.gpsimd.memset(ident[:], 0.0).then_inc(zeroed, 1)
            nc.gpsimd.memset(center[:], -1.0 / D).then_inc(zeroed, 1)
            pool.wait_ge(zeroed, 2)
            nc.gpsimd.affine_select(out=ident[:], in_=ident[:], compare_op=ALU.not_equal, fill=1.0, base=0,
                                    pattern=[[-1, P]], channel_multiplier=1).then_inc(const_made, 1)
            nc.gpsimd.affine_select(out=center[:], in_=center[:], compare_op=ALU.not_equal, fill=1.0 - 1.0 / D,
                                    base=0, pattern=[[-1, P]], channel_multiplier=1).then_inc(const_made, 1)
            nc.gpsimd.memset(k_diag[:], 0.0).then_inc(const_made, 1)
            nc.gpsimd.memset(v_diag[:], 0.0).then_inc(const_made, 1)
            nc.gpsimd.memset(minus_half[:], -0.5).then_inc(const_made, 1)
            nc.gpsimd.iota(expert_no[:], pattern=[[1, E]], base=0, channel_multiplier=0,
                           allow_small_or_imprecise_dtypes=True).then_inc(const_made, 1)
            nc.gpsimd.memset(acc[:], 0.0).then_inc(acc_done, 1)

            def split_rest(raw, hi, lo, raw_in, raw_value, hi_value, free=None):
                pool.wait_ge(raw_in, raw_value)
                pool.wait_ge(w_hi_done, hi_value)
                if free:
                    pool.wait_ge(*free)
                nc.gpsimd.tensor_tensor(lo, raw, hi.bitcast(F32), ALU.subtract).then_inc(w_lo_done, 1)

            def rest_gate_up(k, i, free=None):
                split_rest(raw_gu[:, k], gu_hi[:, k], gu_lo[:, k], in_gu[k], (i + 1) * 32, i * 4 + (k + 1), free)

            def rest_down(k, i, free=None):
                split_rest(raw_d[:, k], d_hi[:, k], d_lo[:, k], in_d[k], (i + 1) * 16, i * 4 + (k + 3), free)

            for b in range(B):
                pool.wait_ge(ln1, 2 * b + 1)
                pool.wait_ge(const_made, 5)
                nc.gpsimd.tensor_tensor(rstd[:, b], var_eps[:, b], minus_half[:], ALU.pow).then_inc(pow1, 1)
            pool.wait_ge(bias_made, 1)
            for b in range(B):
                pool.wait_ge(in_x[b], 16)
                nc.gpsimd.tensor_tensor(x_bias[:, b], x_sb[:, b],
                                        bo_sb[:].unsqueeze(1).broadcast_to([P, T, D]), ALU.add).then_inc(bias_made, 1)

            def normalise(p):
                pool.wait_ge(exp_made, 2 * p + 2)
                pool.wait_ge(inv_made, p + 1)
                if p >= 2:
                    pool.wait_ge(probsT_made, p - 1)
                nc.gpsimd.tensor_tensor(
                    probs[:, p % 2].rearrange("p t (h m) -> p (t h) m", m=M),
                    expd[:, p % 2].rearrange("p t (h m) -> p (t h) m", m=M),
                    row_inv[:, p % 2].unsqueeze(2).broadcast_to([P, 2 * HEADS, M]), ALU.mult).then_inc(probs_made, 1)

            for p in range(NT // 2):
                normalise(p)
                if p == 0:
                    rest_gate_up(0, 0)
                    rest_gate_up(1, 0)
                if p == 2:
                    rest_down(0, 0)
                    rest_down(1, 0)
                if p % 2 == 1:
                    b = p // 2
                    pool.wait_ge(ln2, b + 1)
                    nc.gpsimd.tensor_tensor(rstd2[:, b], var_eps2[:, b], minus_half[:], ALU.pow).then_inc(pow2, 1)

            def add_pair(q, first=0):
                half = (q // EP) % B
                pool.wait_ge(weighted_done, first + (q + 1))
                pool.wait_ge(acc_done, first + (q + 1))
                nc.gpsimd.tensor_tensor(acc[:, half], acc[:, half], weighted[:, q % 2], ALU.add).then_inc(acc_done, 1)

            def unit(n, j=0, last=False):
                if n == HEADSTART and not last:
                    rest_gate_up(0, j + 1, (up_done, j * UNITS + (UNITS - 2)))
                if n == UNITS:
                    rest_gate_up(1, j + 1, (up_done, j * UNITS + UNITS))
                    rest_down(0, j + 1, (down_done, j * UNITS + (UNITS - 2)))
                if n == UNITS + 2:
                    rest_down(1, j + 1, (down_done, j * UNITS + UNITS))
                if n % 2 == 0 and n >= 4:
                    add_pair(n // 2 - 2, j * PAIRS)

            for n in range(HEADSTART):
                unit(n)
            with pool.Fori(0, ROUNDS - 1) as j:
                for n in range(HEADSTART, HEADSTART + UNITS):
                    unit(n, j)
            for q in range(ROUNDS * PAIRS - 3, ROUNDS * PAIRS):
                add_pair(q)

        @block.scalar
        def _(act):
            act.dma_start(wq_sb[:], Wq).then_inc(in_wq, 16)
            act.dma_start(rw_sb[:], router_w).then_inc(in_rw, 16)
            act.dma_start(g_raw[:, 0:1], g_xattn.rearrange("(a n) -> a n", a=1).broadcast_to([P, 1])).then_inc(in_g, 16)
            act.dma_start(g_raw[:, 1:2], g_ffn.rearrange("(a n) -> a n", a=1).broadcast_to([P, 1])).then_inc(in_g, 16)
            act.dma_start(wo_sb[:], Wo_rows).then_inc(in_wo, 16)
            act.dma_start(bo_sb[:], bo.rearrange("(a n) -> a n", a=1).broadcast_to([P, D])).then_inc(in_bo, 16)

            act.wait_ge(in_g, 32)
            nc.scalar.activation(g_tanh[:], g_raw[:], ACT.Tanh).then_inc(tanh_made, 1)
            act.wait_ge(xT_made, 1)
            nc.scalar.activation(xT[:, 0:T], bank[0][:], ACT.Copy).then_inc(xT_out, 1)
            act.wait_ge(wqT_made, 1)
            nc.scalar.activation(wqT[:], bank[6][:], ACT.Copy).then_inc(wqT_out, 1)
            act.wait_ge(xT_made, 2)
            nc.scalar.activation(xT[:, T:NT], bank[1][:], ACT.Copy).then_inc(xT_out, 1)
            act.wait_ge(m_made, 1)
            nc.scalar.activation(m_sb[:].rearrange("p b h m -> p h b m"),
                                 bank[4][:].rearrange("p (h b m) -> p h b m", b=B, m=M), ACT.Copy).then_inc(m_out, 1)

            def round_gate_up(k, i, free=None):
                act.wait_ge(in_gu[k], (i + 1) * 32)
                if free:
                    act.wait_ge(*free)
                nc.scalar.activation(gu_hi[:, k], raw_gu[:, k], ACT.Copy).then_inc(w_hi_done, 1)

            def round_down(k, i, free=None):
                act.wait_ge(in_d[k], (i + 1) * 16)
                if free:
                    act.wait_ge(*free)
                nc.scalar.activation(d_hi[:, k], raw_d[:, k], ACT.Copy).then_inc(w_hi_done, 1)

            round_gate_up(0, 0)
            round_gate_up(1, 0)
            round_down(0, 0)
            round_down(1, 0)

            def exponentials(p):
                act.wait_ge(shift_made, p + 1)
                act.wait_ge(ln1, 2 * (p // 2) + 2)
                if p >= 2:
                    act.wait_ge(probs_made, p - 1)
                for t in range(2):
                    nc.scalar.activation(expd[:, p % 2, t], shifted[:, p % 2, t], ACT.Exp,
                                         scale=rstd_scale[:, 2 * p + t:2 * p + t + 1]).then_inc(exp_made, 1)

            def probsT_copy(p):
                act.wait_ge(probsT_made, p + 1)
                if p >= 2:
                    act.wait_ge(attn_made, p - 1)
                nc.scalar.activation(probsT[:, p % 2], bank[2 + p % 2][:], ACT.Copy).then_inc(probsT_out, 1)

            def tokens2_round(b):
                act.wait_ge(xn2T_made, b + 1)
                nc.scalar.activation(xn2T_hi[:, b], bank[6][:], ACT.Copy).then_inc(xn2_hi_made, 1)

            def router_exp(b):
                act.wait_ge(route, 5 * b + 2)
                nc.scalar.activation(top2_exp[:, b].rearrange("p (t k) -> p t k", k=2),
                                     top8[:, b * T:(b + 1) * T, 0:2], ACT.Exp, scale=-1.0).then_inc(top2_exp_made, 1)

            exponentials(0)
            for p in range(NT // 2):
                if p + 1 < NT // 2:
                    exponentials(p + 1)
                probsT_copy(p)
                if p % 2 == 1:
                    tokens2_round(p // 2)
                    router_exp(p // 2)

            def silu(n, first=0):
                act.wait_ge(gate_done, first + (n + 1))
                if n >= 2:
                    act.wait_ge(hid_done, first + (n - 1))
                nc.scalar.activation(silu_g[:, n % 2], gate_bank[n % 2][:], ACT.Silu).then_inc(silu_done, 1)

            def hid_round(n, first=0):
                act.wait_ge(hid_done, first + (n + 1))
                if n >= 4:
                    act.wait_ge(down_done, first + (n - 3))
                nc.scalar.activation(hid_hi[:, n % 4], hid[:, n % 2], ACT.Copy).then_inc(hid_hi_done, 1)

            def unit(n, j=0, last=False):
                silu(n, j * UNITS)
                hid_round(n, j * UNITS)
                if n == HEADSTART and not last:
                    round_gate_up(0, j + 1, (up_done, j * UNITS + (UNITS - 2)))
                if n == UNITS:
                    round_gate_up(1, j + 1, (up_done, j * UNITS + UNITS))
                    round_down(0, j + 1, (down_done, j * UNITS + (UNITS - 2)))
                if n == UNITS + 2:
                    round_down(1, j + 1, (down_done, j * UNITS + UNITS))

            for n in range(HEADSTART):
                unit(n)
            with act.Fori(0, ROUNDS - 1) as j:
                for n in range(HEADSTART, HEADSTART + UNITS):
                    unit(n, j)
            for n in range(HEADSTART, UNITS):
                unit(n, ROUNDS - 1, last=True)

        @block.vector
        def _(dve):
            for b in range(B):
                dve.wait_ge(in_x[b], 16)
                for t in range(T):
                    nc.vector.bn_stats(stats[:, b * T + t], x_sb[:, b, t]).then_inc(rw_split, 1)
                dve.wait_ge(rw_split, T * (b + 1) + T * b)
                for t in range(T):
                    nc.vector.bn_aggr(mean_var[:, b * T + t], stats[:, b * T + t]).then_inc(rw_split, 1)
                dve.wait_ge(rw_split, 2 * T * (b + 1))
                nc.vector.tensor_scalar(var_eps[:, b], mean_var[:, b * T:(b + 1) * T, 1], LN_EPS, None,
                                        ALU.add).then_inc(ln1, 1)
                if b == 0:
                    dve.wait_ge(small_T, 1)
                    nc.vector.tensor_copy(ctxT[:], bank[7][:, 0:B * M]).then_inc(small_out, 1)
                    nc.vector.tensor_copy(rwT[:], bank[7][:, B * M:B * M + E]).then_inc(small_out, 1)
                    dve.wait_ge(small_out, 2)
                    nc.vector.tensor_copy(rwT_hi[:], rwT[:]).then_inc(small_out, 1)
                    dve.wait_ge(small_out, 3)
                    nc.vector.tensor_tensor(rwT_lo[:], rwT[:], rwT_hi[:].bitcast(F32), ALU.subtract).then_inc(small_out, 1)
                    dve.wait_ge(tanh_made, 1)
                    dve.wait_ge(in_bo, 16)
                    nc.vector.tensor_scalar(bo_sb[:], bo_sb[:], g_tanh[:, 0:1], None, ALU.mult).then_inc(bias_made, 1)
                dve.wait_ge(pow1, b + 1)
                nc.vector.tensor_scalar(rstd_scale[:, b * T:(b + 1) * T], rstd[:, b], SCALE, None,
                                        ALU.mult).then_inc(ln1, 1)
            dve.wait_ge(const_made, 4)
            dve.wait_ge(kv_made, 1)
            for r in range(2):
                rows = slice(DH * r, DH * r + DH)
                nc.vector.tensor_copy(k_diag[rows, :, r],
                                      bank[5][rows, 0:HC * B * M].rearrange("p (c k) -> p c k", c=HC)).then_inc(k_out, 1)
            dve.wait_ge(kv_made, 2)
            for r in range(2):
                rows = slice(DH * r, DH * r + DH)
                v = bank[2][rows, 0:HC * B * M].rearrange("p (j k b m) -> p j k b m", j=2, k=2, b=B)
                for k in range(2):
                    h4 = 2 * k + r
                    nc.vector.tensor_copy(v_diag[rows, :, :, k, h4 * M:(h4 + 1) * M],
                                          v[:, :, k].rearrange("p j b m -> p b j m")).then_inc(v_out, 1)
            dve.wait_ge(u_made, 1)
            nc.vector.tensor_copy(u_sb[:], bank[3][:]).then_inc(u_out, 1)

            def shift(p):
                dve.wait_ge(scores_made, p + 1)
                sc = bank[p % 2][:].rearrange("p (h m) -> p h m", m=M)
                nc.vector.tensor_reduce(row_max[:, p % 2], sc, AX_X, ALU.max).then_inc(max_made, 1)
                dve.wait_ge(max_made, p + 1)
                if p >= 2:
                    dve.wait_ge(exp_made, 2 * p - 2)
                nc.vector.tensor_tensor(shifted[:, p % 2].rearrange("p t (h m) -> p (t h) m", m=M), sc,
                                        row_max[:, p % 2].unsqueeze(2).broadcast_to([P, 2 * HEADS, M]),
                                        ALU.subtract).then_inc(shift_made, 1)

            def sums(p):
                dve.wait_ge(exp_made, 2 * p + 2)
                nc.vector.tensor_reduce(row_sum[:, p % 2], expd[:, p % 2].rearrange("p t (h m) -> p (t h) m", m=M),
                                        AX_X, ALU.add).then_inc(sum_made, 1)
                dve.wait_ge(sum_made, p + 1)
                if p >= 2:
                    dve.wait_ge(probs_made, p - 1)
                nc.vector.reciprocal(row_inv[:, p % 2], row_sum[:, p % 2]).then_inc(inv_made, 1)

            def residual(p):
                b, t = p // 2, 2 * (p % 2)
                dve.wait_ge(attn_made, p + 1)
                dve.wait_ge(bias_made, 2 + b)
                nc.vector.scalar_tensor_tensor(out=x2[:, b, t:t + 2], in0=bank[4 + p % 2][:, 0:2 * D].rearrange("p (t d) -> p t d", t=2),
                                               scalar=g_tanh[:, 0:1], in1=x_bias[:, b, t:t + 2],
                                               op0=ALU.mult, op1=ALU.add).then_inc(x2_made, 1)
                dve.wait_ge(x2_made, p + 1)
                for i in range(2):
                    nc.vector.bn_stats(stats2[:, 2 * p + i], x2[:, b, t + i]).then_inc(stat2_step, 1)
                dve.wait_ge(stat2_step, 4 * p + 2)
                for i in range(2):
                    nc.vector.bn_aggr(mean_var2[:, 2 * p + i], stats2[:, 2 * p + i]).then_inc(stat2_step, 1)
                dve.wait_ge(stat2_step, 4 * p + 4)

            def normalise2(b):
                tiles = slice(b * T, (b + 1) * T)
                nc.vector.tensor_scalar(var_eps2[:, b], mean_var2[:, tiles, 1], LN_EPS, None, ALU.add).then_inc(ln2, 1)
                dve.wait_ge(pow2, b + 1)
                for t in range(T):
                    nc.vector.tensor_scalar(xn2[:, b * T + t], x2[:, b, t], mean_var2[:, b * T + t, 0:1],
                                            rstd2[:, b, t:t + 1], ALU.subtract, ALU.mult).then_inc(xn2_made, 1)
                dve.wait_ge(xn2_hi_made, b + 1)
                nc.vector.tensor_tensor(xn2T_lo[:, b], bank[6][:], xn2T_hi[:, b].bitcast(F32),
                                        ALU.subtract).then_inc(xn2_lo_made, 1)

            def routing(b):
                tiles = slice(b * T, (b + 1) * T)
                dve.wait_ge(logits_made, b + 1)
                nc.vector.tensor_copy(logits[:, tiles], bank[7][:, b * T * E:(b + 1) * T * E].rearrange("p (t e) -> p t e", e=E)).then_inc(route, 1)
                dve.wait_ge(route, 5 * b + 1)
                for t in range(T):
                    top = nc.vector.max(top8[:, b * T + t], logits[:, b * T + t])
                top.then_inc(route, 1)
                dve.wait_ge(route, 5 * b + 2)
                for t in range(T):
                    at = nc.vector.max_index(top8_at[:, b * T + t], top8[:, b * T + t], logits[:, b * T + t])
                at.then_inc(route, 1)
                dve.wait_ge(route, 5 * b + 3)
                nc.vector.tensor_copy(top2_at[:, b].rearrange("p (t k) -> p t k", k=2), top8_at[:, tiles, 0:2]).then_inc(gate_step, 1)
                dve.wait_ge(gate_step, 8 * b + 1)
                dve.wait_ge(const_made, 6)
                nc.vector.tensor_tensor(is_chosen[:, b], expert_no[:].unsqueeze(1).broadcast_to([P, 2 * T, E]),
                                        top2_at[:, b].unsqueeze(2).broadcast_to([P, 2 * T, E]), ALU.is_equal).then_inc(gate_step, 1)
                dve.wait_ge(top2_exp_made, b + 1)
                nc.vector.tensor_scalar(top2_sig[:, b, 0], top2_exp[:, b], 1.0, None, ALU.add).then_inc(gate_step, 1)
                dve.wait_ge(gate_step, 8 * b + 3)
                nc.vector.reciprocal(top2_sig[:, b, 1], top2_sig[:, b, 0]).then_inc(gate_step, 1)
                dve.wait_ge(gate_step, 8 * b + 4)
                sig = top2_sig[:, b, 1].rearrange("p (t k) -> p t k", k=2)
                nc.vector.scalar_tensor_tensor(out=gate_sum[:, b, 0], in0=sig[:, :, 0], scalar=GATE_EPS, in1=sig[:, :, 1],
                                               op0=ALU.add, op1=ALU.add).then_inc(gate_step, 1)
                dve.wait_ge(gate_step, 8 * b + 5)
                nc.vector.reciprocal(gate_sum[:, b, 1], gate_sum[:, b, 0]).then_inc(gate_step, 1)
                dve.wait_ge(gate_step, 8 * b + 6)
                nc.vector.tensor_tensor(top2_sig[:, b, 2].rearrange("p (t k) -> p t k", k=2), sig,
                                        gate_sum[:, b, 1].unsqueeze(2).broadcast_to([P, T, 2]), ALU.mult).then_inc(gate_step, 1)
                dve.wait_ge(gate_step, 8 * b + 7)
                nc.vector.tensor_tensor(is_chosen[:, b], is_chosen[:, b],
                                        top2_sig[:, b, 2].unsqueeze(2).broadcast_to([P, 2 * T, E]), ALU.mult).then_inc(gate_step, 1)
                dve.wait_ge(gate_step, 8 * b + 8)
                both = is_chosen[:, b].rearrange("p (t k) e -> p t k e", k=2)
                nc.vector.tensor_tensor(gates[:, tiles], both[:, :, 0], both[:, :, 1], ALU.add).then_inc(route, 2)
                dve.wait_ge(gatesT_made, b + 1)
                nc.vector.tensor_copy(gatesT[:, b * S:(b + 1) * S], bank[4][0:E, :]).then_inc(gatesT_out, 1)

            shift(0)
            for p in range(NT // 2):
                if p + 1 < NT // 2:
                    shift(p + 1)
                sums(p)
                residual(p)
                if p % 2 == 1:
                    normalise2(p // 2)
                    routing(p // 2)

            def hidden(n, first=0):
                dve.wait_ge(silu_done, first + (n + 1))
                dve.wait_ge(up_done, first + (n + 1))
                if n >= 2:
                    dve.wait_ge(hid_lo_done, first + (n - 1))
                nc.vector.tensor_tensor(hid[:, n % 2], up_bank[n % 2][:], silu_g[:, n % 2], ALU.mult).then_inc(hid_done, 1)

            def hidden_rest(n, first=0):
                dve.wait_ge(hid_hi_done, first + (n + 1))
                nc.vector.tensor_tensor(hid_lo[:, n % 4], hid[:, n % 2], hid_hi[:, n % 4].bitcast(F32),
                                        ALU.subtract).then_inc(hid_lo_done, 1)

            def weigh(q, j=0):
                dve.wait_ge(down_done, j * UNITS + (2 * q + 2))
                dve.wait_ge(in_gate_row[q % PAIRS], (j + (q // PAIRS + 1)) * 16)
                if q >= 1:
                    dve.wait_ge(acc_done, j * PAIRS + q)
                nc.vector.tensor_tensor(weighted[:, q % 2], down_bank[q % 2][:], gate_row[:, q % PAIRS],
                                        ALU.mult).then_inc(weighted_done, 1)

            def unit(n, j=0):
                hidden(n, j * UNITS)
                if n % 2 == 0 and n >= 4:
                    weigh(n // 2 - 2, j)
                hidden_rest(n, j * UNITS)

            for n in range(HEADSTART):
                unit(n)
            with dve.Fori(0, ROUNDS - 1) as j:
                for n in range(HEADSTART, HEADSTART + UNITS):
                    unit(n, j)
            for n in range(HEADSTART, UNITS):
                unit(n, ROUNDS - 1)
            for q in range(ROUNDS * PAIRS - 2, ROUNDS * PAIRS):
                weigh(q)
            for b in range(B):
                dve.wait_ge(accT_made, b + 1)
                nc.vector.scalar_tensor_tensor(out=y[:, b], in0=bank[6 + b][:].rearrange("p (t d) -> p t d", t=T),
                                               scalar=g_tanh[:, 1:2], in1=x2[:, b], op0=ALU.mult, op1=ALU.add).then_inc(y_made, 1)

        @block.tensor
        def _(pe):
            pe.wait_ge(const_made, 2)
            pe.wait_ge(in_ctx, 16)
            nc.tensor.transpose(bank[7][:, 0:B * M], ctx_sb[:], ident[0:B * M, 0:B * M])
            pe.wait_ge(in_rw, 16)
            nc.tensor.transpose(bank[7][:, B * M:B * M + E], rw_sb[:], ident[0:E, 0:E]).then_inc(small_T, 1)
            pe.wait_ge(in_wq, 16)
            for c in range(HC):
                mm = nc.tensor.matmul(bank[6][:, c * D:(c + 1) * D], wq_sb[:, c * P:(c + 1) * P], center[:],
                                      start=True, stop=True)
            mm.then_inc(wqT_made, 1)
            for b in range(B):
                pe.wait_ge(in_x[b], 16)
                for t in range(T):
                    mm = nc.tensor.transpose(bank[b][:, t * P:(t + 1) * P], x_sb[:, b, t], ident[:])
                mm.then_inc(xT_made, 1)
            pe.wait_ge(small_out, 1)
            for w, w_in, bk in ((wk_sb, in_wk, bank[5]), (wv_sb, in_wv, bank[2])):
                pe.wait_ge(w_in, 16)
                for c in range(HC):
                    mm = nc.tensor.matmul(bk[:, c * B * M:(c + 1) * B * M], w[:, c * P:(c + 1) * P],
                                          ctxT[:], start=True, stop=True)
                mm.then_inc(kv_made, 1)
            pe.wait_ge(wqT_out, 1)
            pe.wait_ge(k_out, 2)
            for c in range(HC):
                mm = nc.tensor.matmul(bank[4][:, c * P:(c + 1) * P], wqT[:, c], k_diag[:, c].rearrange("p r k -> p (r k)"),
                                      start=True, stop=True)
            mm.then_inc(m_made, 1)
            pe.wait_ge(v_out, 4)
            pe.wait_ge(in_wo, 16)
            for b in range(B):
                for g in range(2):
                    for k in range(2):
                        mm = nc.tensor.matmul(bank[3][:, (2 * b + g) * D:(2 * b + g + 1) * D], v_diag[:, b, g, k],
                                              wo_sb[:, 2 * g + k], start=(k == 0), stop=(k == 1))
            mm.then_inc(u_made, 1)

            def scores(p):
                b = p // 2
                pe.wait_ge(xT_out, 2)
                pe.wait_ge(m_out, 1)
                if p >= 2:
                    pe.wait_ge(shift_made, p - 1)
                for t in range(2):
                    mm = nc.tensor.matmul(bank[p % 2][:, t * HM:(t + 1) * HM], xT[:, 2 * p + t],
                                          m_sb[:, b].rearrange("p h m -> p (h m)"), start=True, stop=True)
                mm.then_inc(scores_made, 1)

            def turn_probs(p):
                pe.wait_ge(probs_made, p + 1)
                pe.wait_ge(u_out, 1)
                if p >= 2:
                    pe.wait_ge(probsT_out, p - 1)
                for t in range(2):
                    for g in range(2):
                        at = (2 * t + g) * P
                        mm = nc.tensor.transpose(bank[2 + p % 2][:, at:at + P], probs[:, p % 2, t, g * P:(g + 1) * P], ident[:])
                mm.then_inc(probsT_made, 1)

            def attention(p):
                b = p // 2
                pe.wait_ge(probsT_out, p + 1)
                if p >= 2:
                    pe.wait_ge(x2_made, p - 1)
                if p == 2:
                    pe.wait_ge(gatesT_out, 1)
                for t in range(2):
                    for g in range(2):
                        mm = nc.tensor.matmul(bank[4 + p % 2][:, t * D:(t + 1) * D], probsT[:, p % 2, t, g],
                                              u_sb[:, b, g], start=(g == 0), stop=(g == 1))
                mm.then_inc(attn_made, 1)

            def tokens2(b):
                pe.wait_ge(xn2_made, T * (b + 1))
                if b > 0:
                    pe.wait_ge(xn2_lo_made, b)
                for t in range(T):
                    mm = nc.tensor.transpose(bank[6][:, t * P:(t + 1) * P], xn2[:, b * T + t], ident[:])
                mm.then_inc(xn2T_made, 1)
                pe.wait_ge(small_out, 4)
                pe.wait_ge(xn2_lo_made, b + 1)
                if b > 0:
                    pe.wait_ge(route, 5 * b)
                for t in range(T):
                    at = (b * T + t) * E
                    terms = [(xt, w) for xt in (xn2T_hi, xn2T_lo) for w in (rwT_hi, rwT_lo)]
                    for i, (xt, w) in enumerate(terms):
                        mm = nc.tensor.matmul(bank[7][:, at:at + E], xt[:, b, t * P:(t + 1) * P], w[:],
                                              start=(i == 0), stop=(i == len(terms) - 1))
                mm.then_inc(logits_made, 1)

            def turn_gates(b):
                pe.wait_ge(route, 5 * b + 5)
                pe.wait_ge(x2_made, 2 * b + 1)
                for t in range(T):
                    mm = nc.tensor.transpose(bank[4][0:E, t * P:(t + 1) * P], gates[:, b * T + t], ident[:])
                mm.then_inc(gatesT_made, 1)

            scores(0)
            for p in range(NT // 2):
                if p + 1 < NT // 2:
                    scores(p + 1)
                turn_probs(p)
                attention(p)
                if p % 2 == 1:
                    tokens2(p // 2)
                    turn_gates(p // 2)

            def gate_up(n, j=0):
                half, k, c = unit_of(n)
                pe.wait_ge(w_lo_done, (j + n // UNITS) * 4 + (k + 1))
                if n >= 2:
                    pe.wait_ge(hid_done, j * UNITS + (n - 1))
                for i, (bk, done) in enumerate(((gate_bank, gate_done), (up_bank, up_done))):
                    cols = slice(c * P, (c + 1) * P)
                    terms = [(gu_hi, xn2T_hi), (gu_lo, xn2T_hi), (gu_hi, xn2T_lo)]
                    for s, (w, xt) in enumerate(terms):
                        mm = nc.tensor.matmul(bk[n % 2][:], w[:, k, i, cols], xt[:, half],
                                              start=(s == 0), stop=(s == len(terms) - 1))
                    mm.then_inc(done, 1)

            def down(n, j=0):
                half, k, c = unit_of(n)
                q = n // FC
                pe.wait_ge(hid_lo_done, j * UNITS + (n + 1))
                pe.wait_ge(w_lo_done, (j + n // UNITS) * 4 + (k + 3))
                if c == 0 and q >= 2:
                    pe.wait_ge(weighted_done, j * PAIRS + (q - 1))
                terms = [(d_hi, hid_hi), (d_lo, hid_hi), (d_hi, hid_lo)]
                for s, (w, h) in enumerate(terms):
                    mm = nc.tensor.matmul(down_bank[q % 2][:], w[:, k, c], h[:, n % 4],
                                          start=(c == 0 and s == 0), stop=(c == FC - 1 and s == len(terms) - 1))
                mm.then_inc(down_done, 1)

            pe.wait_ge(gatesT_out, 2)
            for n in range(HEADSTART):
                gate_up(n)
                if n >= LAG:
                    down(n - LAG)
            with pe.Fori(0, ROUNDS - 1) as j:
                for n in range(HEADSTART, HEADSTART + UNITS):
                    gate_up(n, j)
                    down(n - LAG, j)
            for n in range(HEADSTART, UNITS):
                gate_up(n, ROUNDS - 1)
                down(n - LAG, ROUNDS - 1)
            for n in range(UNITS - LAG, UNITS):
                down(n, ROUNDS - 1)
            for b in range(B):
                pe.wait_ge(acc_done, 1 + ROUNDS * PAIRS - EP * (B - 1 - b))
                for t in range(T):
                    mm = nc.tensor.transpose(bank[6 + b][:, t * P:(t + 1) * P], acc[:, b, t * P:(t + 1) * P], ident[:])
                mm.then_inc(accT_made, 1)


_INS = ['x', 'ctx_1024', 'g_xattn', 'g_ffn', 'L0_xattn_Wq', 'L0_xattn_Wk', 'L0_xattn_Wv', 'L0_xattn_Wo',
        'L0_xattn_bo', 'L0_ffn_router_w', 'L0_ffn_w_gate', 'L0_ffn_w_up', 'L0_ffn_w_down']
_OUTS = [((2, 512, 128), 'float32')]


def kernel(**inputs):
    import numpy as _np
    import concourse.bacc as _bacc
    from concourse import mybir as _mybir
    from concourse.bass_utils import run_bass_kernel_spmd as _run

    nc = _bacc.Bacc("TRN2", target_bir_lowering=False, num_devices=1)
    arrays, args = {}, []
    for name in _INS:
        a = _np.ascontiguousarray(inputs[name])
        arrays[f"in_{name}_dram"] = a
        args.append(nc.dram_tensor(f"in_{name}_dram", a.shape, _mybir.dt.from_np(a.dtype), kind="ExternalInput").ap())
    for i, (shape, dtype) in enumerate(_OUTS):
        dt = _mybir.dt.from_np(_np.dtype(dtype))
        args.append(nc.dram_tensor(f"out_{i}_dram", shape, dt, kind="ExternalOutput").ap())
    gated_cross_attention_and_top2_experts(nc, *args)
    r = _run(nc, [arrays], core_ids=[0])
    got = tuple(r.results[0][f"out_{i}_dram"] for i in range(len(_OUTS)))
    return got[0]
```

```python
import math
from contextlib import ExitStack

import concourse.bass as bass
from concourse import mybir

P = 128
F32 = mybir.dt.float32
F32R = mybir.dt.float32r
BF16 = mybir.dt.bfloat16
U32 = mybir.dt.uint32
ALU = mybir.AluOpType
ACT = mybir.ActivationFunctionType
AX_X = mybir.AxisListType.X


def gated_cross_attention_and_top2_experts(
    nc: bass.Bass,
    x: bass.AP,
    ctx: bass.AP,
    g_xattn: bass.AP,
    g_ffn: bass.AP,
    Wq: bass.AP,
    Wk: bass.AP,
    Wv: bass.AP,
    Wo: bass.AP,
    bo: bass.AP,
    router_w: bass.AP,
    w_gate: bass.AP,
    w_up: bass.AP,
    w_down: bass.AP,
    out: bass.AP,
):
    B, S, D = x.shape
    M = ctx.shape[1]
    HID = Wq.shape[1]
    DH = 64
    HEADS = HID // DH
    E, _, H = w_gate.shape
    T = S // P
    NT = B * T
    HC = HID // P
    HM = HEADS * M
    FC = H // P
    SCALE = DH ** -0.5
    LN_EPS = 1e-5
    GATE_EPS = 1e-10
    assert D == P and B == 2 and S == 512 and HM == 256 and E == 8 and FC == 2

    EP = 2
    ROUNDS = E // EP
    UNITS = EP * B * FC
    PAIRS = EP * B
    LAG = 2
    HEADSTART = 13

    WARM0, WARM1, WARM2, WARM3, WARM4, WARM5 = 8, 4, 4, 4, 4, 4
    SPREAD_AT = (5, 6, 8, 9)
    TURN_AT = (5, 9)
    LOOPS = ROUNDS - 2
    x_rows = x.rearrange("b (p t) d -> p b t d", t=T)
    out_rows = out.rearrange("b (p t) d -> p b t d", t=T)
    ctx_rows = ctx.rearrange("b m d -> (b m) d")
    Wo_rows = Wo.rearrange("(c k) n -> k c n", k=P)

    with ExitStack() as stack:
        def sb(name, shape, dt=F32):
            return stack.enter_context(nc.sbuf_tensor(name, shape, dt))

        def sem(name):
            return stack.enter_context(nc.semaphore(name))

        bank = [stack.enter_context(nc.psum_tensor(f"bank{i}", [P, 512], F32)) for i in range(8)]
        gates_dram = nc.dram_tensor("gates_dram", [E, B * S], F32, kind="Internal").ap()

        ident = sb("ident", [P, P])
        blank = sb("blank", [P, 512], BF16)
        center = sb("center", [P, P])
        expert_no = sb("expert_no", [P, E])
        minus_half = sb("minus_half", [P, T])
        inv_e = sb("inv_e", [P, 2 * T])
        x_sb = sb("x_sb", [P, B, T, D])
        ctx_sb = sb("ctx_sb", [B * M, D])
        wq_sb = sb("wq_sb", [P, HID])
        wk_sb = sb("wk_sb", [P, HID])
        wv_sb = sb("wv_sb", [P, HID])
        wo_sb = sb("wo_sb", [P, HC, D])
        bo_sb = sb("bo_sb", [P, D])
        rw_sb = sb("rw_sb", [E, D])
        g_raw = sb("g_raw", [P, 2])
        g_tanh = sb("g_tanh", [P, 2])
        ctxT = sb("ctxT", [P, B * M])
        rwT = sb("rwT", [P, E])
        rwT_parts = sb("rwT_parts", [P, 2, E], F32R)
        wqT = sb("wqT", [P, HC, D])
        k_diag = sb("k_diag", [P, HC, 2, B * M])
        v_diag = sb("v_diag", [P, B, 2, 2, P])
        m_sb = sb("m_sb", [P, B, HEADS, M])
        u_sb = sb("u_sb", [P, B, 2, D])
        xT = sb("xT", [P, NT, P])
        stats = sb("stats", [P, NT, 6])
        mean_var = sb("mean_var", [P, NT, 2])
        var_eps = sb("var_eps", [P, B, T])
        rstd = sb("rstd", [P, B, T])
        rstd_scale = sb("rstd_scale", [P, NT])
        x_bias = sb("x_bias", [P, B, T, D])
        row_max = sb("row_max", [P, 2, 2 * HEADS])
        shifted = sb("shifted", [P, 2, 2, HM])
        expd = sb("expd", [P, 2, 2, HM])
        row_sum = sb("row_sum", [P, 2, 2 * HEADS])
        row_inv = sb("row_inv", [P, 2, 2 * HEADS])
        probs = sb("probs", [P, 2, 2, HM])
        probsT = sb("probsT", [P, 2, 2, 2, P])
        x2 = sb("x2", [P, B, T, D])
        stats2 = sb("stats2", [P, NT, 6])
        mean_var2 = sb("mean_var2", [P, NT, 2])
        var_eps2 = sb("var_eps2", [P, B, T])
        rstd2 = sb("rstd2", [P, B, T])
        xn2 = sb("xn2", [P, NT, D])
        xn2T_hi = sb("xn2T_hi", [P, B, S], F32R)
        xn2T_lo = sb("xn2T_lo", [P, B, S], F32R)
        logits = sb("logits", [P, NT, E])
        top8 = sb("top8", [P, NT, 8])
        top8_at = sb("top8_at", [P, NT, 8], U32)
        top2_exp = sb("top2_exp", [P, B, 2, 2 * T])
        top2_sig = sb("top2_sig", [P, B, 2, 2 * T])
        gate_sum = sb("gate_sum", [P, B, 3, T])
        is_chosen = sb("is_chosen", [P, B, 2 * T, E])
        chosen_gate = sb("chosen_gate", [P, B, 2 * T, E])
        gates = sb("gates", [P, NT, E])
        gatesT = sb("gatesT", [E, B * S])
        raw_gu = sb("raw_gu", [P, EP, 2, H])
        raw_d = sb("raw_d", [P, EP, FC, D])
        gu_hi = sb("gu_hi", [P, EP, 2, H], F32R)
        gu_lo = sb("gu_lo", [P, EP, 2, H], F32R)
        d_hi = sb("d_hi", [P, EP, FC, D], F32R)
        d_lo = sb("d_lo", [P, EP, FC, D], F32R)
        silu_g = sb("silu_g", [P, 2, S])
        hid = sb("hid", [P, 2, S])
        hid_hi = sb("hid_hi", [P, 4, S], F32R)
        hid_lo = sb("hid_lo", [P, 4, S], F32R)
        gate_row = sb("gate_row", [P, PAIRS, S])
        weighted = sb("weighted", [P, 2, S])
        acc = sb("acc", [P, B, S])
        y = sb("y", [P, B, T, D])

        in_x = [sem(f"in_x{b}") for b in range(B)]
        in_ctx, in_wq, in_wk, in_wv, in_wo = (sem(f"in_{n}") for n in ("ctx", "wq", "wk", "wv", "wo"))
        in_bo, in_rw, in_g = sem("in_bo"), sem("in_rw"), sem("in_g")
        in_gu = [sem(f"in_gu{i}") for i in range(EP)]
        in_d = [sem(f"in_d{i}") for i in range(EP)]
        in_gate_row = [sem(f"in_gate_row{i}") for i in range(PAIRS)]
        gates_stored = [sem(f"gates_stored{b}") for b in range(B)]
        out_stored = [sem(f"out_stored{b}") for b in range(B)]
        zeroed, blank_made = sem("zeroed"), sem("blank_made")
        ident_made, center_made = sem("ident_made"), sem("center_made")
        k_zeroed, v_zeroed = sem("k_zeroed"), sem("v_zeroed")
        const_made = sem("const_made")
        ctxT_made, ctxT_out = sem("ctxT_made"), sem("ctxT_out")
        rwT_made, rwT_out = sem("rwT_made"), sem("rwT_out")
        wqT_made, wqT_out = sem("wqT_made"), sem("wqT_out")
        k_made, v_made, k_out, v_out = sem("k_made"), sem("v_made"), sem("k_out"), sem("v_out")
        m_made, m_out, u_made, u_out = sem("m_made"), sem("m_out"), sem("u_made"), sem("u_out")
        xT_made, xT_out = sem("xT_made"), sem("xT_out")
        tanh_made = sem("tanh_made")
        bo_scaled, bias_made = sem("bo_scaled"), sem("bias_made")
        stat1_step, var1_made, pow1, scale1_made = (
            sem("stat1_step"), sem("var1_made"), sem("pow1"), sem("scale1_made"))
        scores_made, shift_made, exp_made = sem("scores_made"), sem("shift_made"), sem("exp_made")
        max_made, stat2_step = sem("max_made"), sem("stat2_step")
        sum_made, inv_made = sem("sum_made"), sem("inv_made")
        probs_made = [sem(f"probs_made{p}") for p in range(NT // 2)]
        probsT_made, probsT_out = sem("probsT_made"), sem("probsT_out")
        attn_made, x2_made = sem("attn_made"), sem("x2_made")
        ln2, pow2, xn2_made = sem("ln2"), sem("pow2"), sem("xn2_made")
        xn2T_made, xn2_hi_made, xn2_lo_made = sem("xn2T_made"), sem("xn2_hi_made"), sem("xn2_lo_made")
        logits_made, logits_out = sem("logits_made"), sem("logits_out")
        top8_made, top8_at_made, chosen_made, gate_step, gates_made = (
            sem("top8_made"), sem("top8_at_made"), sem("chosen_made"), sem("gate_step"), sem("gates_made"))
        gate_exp_made = sem("gate_exp_made")
        spread_made, gate_spread = sem("spread_made"), sem("gate_spread")
        gatesT_made, gatesT_out = sem("gatesT_made"), sem("gatesT_out")
        w_hi_done, w_lo_done = sem("w_hi_done"), sem("w_lo_done")
        gate_done, up_done, down_done = sem("gate_done"), sem("up_done"), sem("down_done")
        silu_done, hid_done, hid_hi_done, hid_lo_done = (
            sem("silu_done"), sem("hid_done"), sem("hid_hi_done"), sem("hid_lo_done"))
        weighted_done, acc_done = sem("weighted_done"), sem("acc_done")
        accT_made, y_made = sem("accT_made"), sem("y_made")

        gate_bank, up_bank, down_bank = bank[0:2], bank[2:4], bank[4:6]
        probsT_bank = [bank[2], bank[3], bank[6], bank[7]]
        attn_bank = [bank[4], bank[5], bank[6], bank[7]]
        logits_bank = [bank[5], bank[7]]
        gatesT_bank = [bank[7], bank[7]]
        spread_bank = [bank[6], bank[6]]

        def unit_of(n):
            m = n % UNITS
            return m // (EP * FC), (m // FC) % EP, m % FC

        def normalise(eng, p):
            eng.wait_ge(exp_made, 2 * p + 2)
            eng.wait_ge(inv_made, p + 1)
            if p >= 2:
                eng.wait_ge(probsT_made, p - 1)
            eng.tensor_tensor(
                probs[:, p % 2].rearrange("p t (h m) -> p (t h) m", m=M),
                expd[:, p % 2].rearrange("p t (h m) -> p (t h) m", m=M),
                row_inv[:, p % 2].unsqueeze(2).broadcast_to([P, 2 * HEADS, M]), ALU.mult).then_inc(probs_made[p], 1)

        block = stack.enter_context(nc.Block())

        @block.sync
        def _(sp):
            sp.dma_start(ctx_sb[:], ctx_rows).then_inc(in_ctx, 16)
            sp.dma_start(wq_sb[:], Wq).then_inc(in_wq, 16)
            sp.dma_start(wv_sb[:], Wv).then_inc(in_wv, 16)
            sp.dma_start(wo_sb[:], Wo_rows).then_inc(in_wo, 16)
            sp.dma_start(g_raw[:, 0:1], g_xattn.rearrange("(a n) -> a n", a=1).broadcast_to([P, 1])).then_inc(in_g, 16)
            sp.dma_start(g_raw[:, 1:2], g_ffn.rearrange("(a n) -> a n", a=1).broadcast_to([P, 1])).then_inc(in_g, 16)
            sp.dma_start(x_sb[:, 1], x_rows[:, 1]).then_inc(in_x[1], 16)
            sp.dma_start(rw_sb[:], router_w).then_inc(in_rw, 16)
            sp.dma_start(bo_sb[:], bo.rearrange("(a n) -> a n", a=1).broadcast_to([P, D])).then_inc(in_bo, 16)

            def load_gate_up(e, k):
                for i, w in enumerate((w_gate, w_up)):
                    sp.dma_start(raw_gu[:, k, i], w[bass.ds(e, 1)].rearrange("a d h -> (a d) h")).then_inc(in_gu[k], 16)

            def load_down(e, k):
                sp.dma_start(raw_d[:, k], w_down[bass.ds(e, 1)].rearrange("a (c p) d -> (a p) c d", p=P)
                             ).then_inc(in_d[k], 16)

            for k in range(EP):
                load_gate_up(k, k)
            for k in range(EP):
                load_down(k, k)

            def load_gate_row(e, q):
                half, k = q // EP, q % EP
                src = gates_dram[bass.ds(e, 1), half * S:(half + 1) * S]
                sp.dma_start(gate_row[:, q], src.broadcast_to([P, S])).then_inc(in_gate_row[q], 16)

            def pass_gates(b):
                sp.wait_ge(gatesT_out, b + 1)
                sp.dma_start(gates_dram[:, b * S:(b + 1) * S], gatesT[:, b * S:(b + 1) * S]
                             ).then_inc(gates_stored[b], 16)

            def next_weights(i, r):
                sp.wait_ge(w_lo_done, r * 4 + (i + 1))
                load = load_gate_up if i < EP else load_down
                load(r * EP + (EP + i % EP), i % EP)

            def next_gate_row(q, r):
                sp.wait_ge(weighted_done, r * PAIRS + (q + 1))
                load_gate_row(r * EP + (EP + q % EP), q)

            next_weights(0, 0)
            next_weights(1, 0)
            pass_gates(0)
            next_weights(2, 0)
            next_weights(3, 0)
            pass_gates(1)
            for b in range(B):
                sp.wait_ge(gates_stored[b], 16)
            with sp.Fori(0, LOOPS) as j:
                for q in range(PAIRS):
                    next_weights(q, j + 1)
                    next_gate_row(q, j)
            for q in range(PAIRS):
                next_gate_row(q, ROUNDS - 2)
            for b in range(B):
                sp.wait_ge(y_made, b + 1)
                sp.dma_start(out_rows[:, b], y[:, b]).then_inc(out_stored[b], 16)
            for b in range(B):
                sp.wait_ge(out_stored[b], 16)

        @block.gpsimd
        def _(pool):
            nc.gpsimd.memset(ident[:], 0.0).then_inc(zeroed, 1)
            pool.wait_ge(zeroed, 1)
            nc.gpsimd.affine_select(out=ident[:], in_=ident[:], compare_op=ALU.not_equal, fill=1.0, base=0,
                                    pattern=[[-1, P]], channel_multiplier=1).then_inc(ident_made, 1)
            nc.gpsimd.memset(center[:], -1.0 / D).then_inc(zeroed, 1)
            pool.wait_ge(zeroed, 2)
            nc.gpsimd.affine_select(out=center[:], in_=center[:], compare_op=ALU.not_equal, fill=1.0 - 1.0 / D,
                                    base=0, pattern=[[-1, P]], channel_multiplier=1).then_inc(center_made, 1)
            nc.gpsimd.memset(k_diag[:], 0.0).then_inc(k_zeroed, 1)
            nc.gpsimd.memset(v_diag[:], 0.0).then_inc(v_zeroed, 1)
            nc.gpsimd.memset(minus_half[:], -0.5).then_inc(const_made, 1)
            nc.gpsimd.memset(inv_e[:], math.exp(-1.0)).then_inc(const_made, 1)
            nc.gpsimd.iota(expert_no[:], pattern=[[1, E]], base=0, channel_multiplier=0,
                           allow_small_or_imprecise_dtypes=True).then_inc(const_made, 1)

            def split_rest(raw, hi, lo, raw_in, raw_value, hi_value, free=None):
                pool.wait_ge(raw_in, raw_value)
                pool.wait_ge(w_hi_done, hi_value)
                if free:
                    pool.wait_ge(*free)
                nc.gpsimd.tensor_tensor(lo, raw, hi.bitcast(F32), ALU.subtract).then_inc(w_lo_done, 1)

            def rest_gate_up(k, i, free=None):
                split_rest(raw_gu[:, k], gu_hi[:, k], gu_lo[:, k], in_gu[k], (i + 1) * 32, i * 4 + (k + 1), free)

            def rest_down(k, i, free=None):
                split_rest(raw_d[:, k], d_hi[:, k], d_lo[:, k], in_d[k], (i + 1) * 16, i * 4 + (k + 3), free)

            def inv_std(b):
                pool.wait_ge(var1_made, b + 1)
                pool.wait_ge(const_made, 1)
                nc.gpsimd.tensor_tensor(rstd[:, b], var_eps[:, b], minus_half[:], ALU.pow).then_inc(pow1, 1)

            def add_bias(b):
                pool.wait_ge(bo_scaled, 1)
                pool.wait_ge(in_x[b], 16)
                nc.gpsimd.tensor_tensor(x_bias[:, b], x_sb[:, b],
                                        bo_sb[:].unsqueeze(1).broadcast_to([P, T, D]), ALU.add).then_inc(bias_made, 1)

            def inv_std2(b):
                pool.wait_ge(ln2, b + 1)
                nc.gpsimd.tensor_tensor(rstd2[:, b], var_eps2[:, b], minus_half[:], ALU.pow).then_inc(pow2, 1)

            def gate_exp(b):
                pool.wait_ge(const_made, 2)
                pool.wait_ge(top8_made, b + 1)
                nc.gpsimd.tensor_tensor(top2_exp[:, b, 0].rearrange("p (t k) -> p t k", k=2),
                                        inv_e[:].rearrange("p (t k) -> p t k", k=2),
                                        top8[:, b * T:(b + 1) * T, 0:2], ALU.pow).then_inc(gate_exp_made, 1)

            def add_pair(q, first=0):
                half = (q // EP) % B
                pool.wait_ge(weighted_done, first + (q + 1))
                pool.wait_ge(acc_done, first + (q + 2))
                nc.gpsimd.tensor_tensor(acc[:, half], acc[:, half], weighted[:, q % 2], ALU.add).then_inc(acc_done, 1)

            def unit(n, j):
                turn, m = n // UNITS, n % UNITS
                if m == 5:
                    rest_gate_up(0, j + (turn + 1), (up_done, j * UNITS + (n + 1)))
                if m == 7:
                    rest_gate_up(1, j + (turn + 1), (up_done, j * UNITS + (n + 1)))
                if m == 0:
                    rest_down(0, j + turn, (down_done, j * UNITS + (n - LAG)))
                if m == 2:
                    rest_down(1, j + turn, (down_done, j * UNITS + (n - LAG)))
                if n % 2 == 1:
                    add_pair((n - 5) // 2, j * PAIRS)

            inv_std(0)
            inv_std(1)
            add_bias(0)
            rest_gate_up(0, 0)
            add_bias(1)
            rest_gate_up(1, 0)
            inv_std2(0)
            normalise(pool, 2)
            normalise(pool, 3)
            rest_down(0, 0)
            rest_down(1, 0)
            inv_std2(1)
            gate_exp(0)
            for b in range(B):
                nc.gpsimd.memset(acc[:, b], 0.0).then_inc(acc_done, 1)
            gate_exp(1)
            for n in range(5, HEADSTART):
                unit(n, 0)
            with pool.Fori(0, LOOPS) as j:
                for n in range(HEADSTART, HEADSTART + UNITS):
                    unit(n, j)
            for q in range(ROUNDS * PAIRS - 4, ROUNDS * PAIRS):
                add_pair(q)

        @block.scalar
        def _(act):
            act.dma_start(wk_sb[:], Wk).then_inc(in_wk, 16)
            act.dma_start(x_sb[:, 0], x_rows[:, 0]).then_inc(in_x[0], 16)
            nc.scalar.preload_act_table(ACT.Exp)

            act.wait_ge(wqT_made, 1)
            nc.scalar.activation(wqT[:], bank[6][:], ACT.Copy).then_inc(wqT_out, 1)
            act.wait_ge(xT_made, 1)
            nc.scalar.activation(xT[:, 0:T], bank[2][:], ACT.Copy).then_inc(xT_out, 1)
            act.wait_ge(m_made, 1)
            nc.scalar.activation(m_sb[:].rearrange("p b h m -> p h b m"),
                                 bank[4][:].rearrange("p (h b m) -> p h b m", b=B, m=M), ACT.Copy).then_inc(m_out, 1)
            act.wait_ge(in_g, 32)
            nc.scalar.activation(g_tanh[:], g_raw[:], ACT.Tanh).then_inc(tanh_made, 1)
            act.wait_ge(xT_made, 2)
            nc.scalar.activation(xT[:, T:NT], bank[3][:], ACT.Copy).then_inc(xT_out, 1)

            def round_gate_up(k, i, free=None):
                act.wait_ge(in_gu[k], (i + 1) * 32)
                if free:
                    act.wait_ge(*free)
                nc.scalar.activation(gu_hi[:, k], raw_gu[:, k], ACT.Copy).then_inc(w_hi_done, 1)

            def round_down(k, i, free=None):
                act.wait_ge(in_d[k], (i + 1) * 16)
                if free:
                    act.wait_ge(*free)
                nc.scalar.activation(d_hi[:, k], raw_d[:, k], ACT.Copy).then_inc(w_hi_done, 1)

            round_gate_up(0, 0)

            def exponentials(p):
                act.wait_ge(shift_made, p + 1)
                act.wait_ge(scale1_made, p // 2 + 1)
                if p >= 2:
                    act.wait_ge(probs_made[p - 2], 1)
                for t in range(2):
                    nc.scalar.activation(expd[:, p % 2, t], shifted[:, p % 2, t], ACT.Exp,
                                         scale=rstd_scale[:, 2 * p + t:2 * p + t + 1]).then_inc(exp_made, 1)

            def probsT_copy(p):
                act.wait_ge(probsT_made, p + 1)
                if p >= 2:
                    act.wait_ge(attn_made, p - 1)
                nc.scalar.activation(probsT[:, p % 2], probsT_bank[p][:], ACT.Copy).then_inc(probsT_out, 1)

            def tokens2_round(b):
                act.wait_ge(xn2T_made, b + 1)
                nc.scalar.activation(xn2T_hi[:, b], bank[6][:], ACT.Copy).then_inc(xn2_hi_made, 1)

            act.wait_ge(u_made, 1)
            nc.scalar.activation(u_sb[:], bank[5][:], ACT.Copy).then_inc(u_out, 1)
            exponentials(0)
            exponentials(1)
            round_gate_up(1, 0)
            round_down(0, 0)
            probsT_copy(0)
            probsT_copy(1)
            exponentials(2)
            round_down(1, 0)
            exponentials(3)
            nc.scalar.preload_act_table(ACT.Silu)
            tokens2_round(0)

            def silu(n, first=0):
                act.wait_ge(gate_done, first + (n + 1))
                if n >= 2:
                    act.wait_ge(hid_done, first + (n - 1))
                nc.scalar.activation(silu_g[:, n % 2], gate_bank[n % 2][:], ACT.Silu).then_inc(silu_done, 1)

            def hid_round(n, first=0):
                act.wait_ge(hid_done, first + (n + 1))
                if n >= 4:
                    act.wait_ge(down_done, first + (n - 3))
                nc.scalar.activation(hid_hi[:, n % 4], hid[:, n % 2], ACT.Copy).then_inc(hid_hi_done, 1)

            def unit(n, j=0, last=False):
                silu(n, j * UNITS)
                turn, m = n // UNITS, n % UNITS
                if m == 5 and not last:
                    round_gate_up(0, j + (turn + 1), (up_done, j * UNITS + (n + 1)))
                if m == 7 and not last:
                    round_gate_up(1, j + (turn + 1), (up_done, j * UNITS + (n + 1)))
                if m == 0 and n > 0:
                    round_down(0, j + turn, (down_done, j * UNITS + (n - LAG)))
                if m == 2 and n > 2:
                    round_down(1, j + turn, (down_done, j * UNITS + (n - LAG)))
                hid_round(n, j * UNITS)

            def spread_copy(q):
                act.wait_ge(spread_made, q + 1)
                nc.scalar.activation(gate_row[:, q], spread_bank[q // EP][:], ACT.Copy).then_inc(gate_spread, 1)

            silu(0)
            probsT_copy(2)
            hid_round(0)
            probsT_copy(3)
            for n in range(1, HEADSTART):
                unit(n)
                if n == 3:
                    tokens2_round(1)
                if n + 1 in SPREAD_AT:
                    spread_copy(SPREAD_AT.index(n + 1))
            with act.Fori(0, LOOPS) as j:
                for n in range(HEADSTART, HEADSTART + UNITS):
                    unit(n, j)
            for n in range(ROUNDS * UNITS - 3, ROUNDS * UNITS):
                unit(n, last=True)

        @block.vector
        def _(dve):
            nc.vector.memset(blank[:], 0.0).then_inc(blank_made, 1)

            def statistics(b):
                dve.wait_ge(in_x[b], 16)
                for t in range(T):
                    nc.vector.bn_stats(stats[:, b * T + t], x_sb[:, b, t]).then_inc(stat1_step, 1)
                dve.wait_ge(stat1_step, 2 * T * b + T)
                for t in range(T):
                    nc.vector.bn_aggr(mean_var[:, b * T + t], stats[:, b * T + t]).then_inc(stat1_step, 1)
                dve.wait_ge(stat1_step, 2 * T * b + 2 * T)
                nc.vector.tensor_scalar(var_eps[:, b], mean_var[:, b * T:(b + 1) * T, 1], LN_EPS, None,
                                        ALU.add).then_inc(var1_made, 1)

            def exp_scale(b):
                dve.wait_ge(pow1, b + 1)
                nc.vector.tensor_scalar(rstd_scale[:, b * T:(b + 1) * T], rstd[:, b], SCALE, None,
                                        ALU.mult).then_inc(scale1_made, 1)

            dve.wait_ge(ctxT_made, 1)
            nc.vector.tensor_copy(ctxT[:], bank[7][:, 0:B * M]).then_inc(ctxT_out, 1)
            dve.wait_ge(k_zeroed, 1)
            dve.wait_ge(k_made, 1)
            for r in range(2):
                rows = slice(DH * r, DH * r + DH)
                nc.vector.tensor_copy(k_diag[rows, :, r],
                                      bank[5][rows, 0:HC * B * M].rearrange("p (c k) -> p c k", c=HC)).then_inc(k_out, 1)
            statistics(0)
            dve.wait_ge(v_zeroed, 1)
            dve.wait_ge(v_made, 1)
            for r in range(2):
                rows = slice(DH * r, DH * r + DH)
                v = bank[7][rows, 0:HC * B * M].rearrange("p (j k b m) -> p j k b m", j=2, k=2, b=B)
                for k in range(2):
                    h4 = 2 * k + r
                    nc.vector.tensor_copy(v_diag[rows, :, :, k, h4 * M:(h4 + 1) * M],
                                          v[:, :, k].rearrange("p j b m -> p b j m")).then_inc(v_out, 1)
            statistics(1)
            exp_scale(0)
            dve.wait_ge(tanh_made, 1)
            dve.wait_ge(in_bo, 16)
            nc.vector.tensor_scalar(bo_sb[:], bo_sb[:], g_tanh[:, 0:1], None, ALU.mult).then_inc(bo_scaled, 1)

            def split_router():
                dve.wait_ge(rwT_made, 1)
                nc.vector.tensor_copy(rwT[:], bank[6][:, 0:E]).then_inc(rwT_out, 1)
                dve.wait_ge(rwT_out, 1)
                nc.vector.tensor_copy(rwT_parts[:, 0], rwT[:]).then_inc(rwT_out, 1)
                dve.wait_ge(rwT_out, 2)
                nc.vector.tensor_tensor(rwT_parts[:, 1], rwT[:], rwT_parts[:, 0].bitcast(F32),
                                        ALU.subtract).then_inc(rwT_out, 1)

            def shift(p):
                dve.wait_ge(scores_made, p + 1)
                sc = bank[p % 2][:].rearrange("p (h m) -> p h m", m=M)
                nc.vector.tensor_reduce(row_max[:, p % 2], sc, AX_X, ALU.max).then_inc(max_made, 1)
                dve.wait_ge(max_made, p + 1)
                if p >= 2:
                    dve.wait_ge(exp_made, 2 * p - 2)
                nc.vector.tensor_tensor(shifted[:, p % 2].rearrange("p t (h m) -> p (t h) m", m=M), sc,
                                        row_max[:, p % 2].unsqueeze(2).broadcast_to([P, 2 * HEADS, M]),
                                        ALU.subtract).then_inc(shift_made, 1)

            def sums(p):
                dve.wait_ge(exp_made, 2 * p + 2)
                nc.vector.tensor_reduce(row_sum[:, p % 2], expd[:, p % 2].rearrange("p t (h m) -> p (t h) m", m=M),
                                        AX_X, ALU.add).then_inc(sum_made, 1)
                dve.wait_ge(sum_made, p + 1)
                if p >= 2:
                    dve.wait_ge(probs_made[p - 2], 1)
                nc.vector.reciprocal(row_inv[:, p % 2], row_sum[:, p % 2]).then_inc(inv_made, 1)

            def residual(p):
                b, t = p // 2, 2 * (p % 2)
                dve.wait_ge(attn_made, p + 1)
                dve.wait_ge(bias_made, 1 + b)
                nc.vector.scalar_tensor_tensor(out=x2[:, b, t:t + 2], in0=attn_bank[p][:, 0:2 * D].rearrange("p (t d) -> p t d", t=2),
                                               scalar=g_tanh[:, 0:1], in1=x_bias[:, b, t:t + 2],
                                               op0=ALU.mult, op1=ALU.add).then_inc(x2_made, 1)
                dve.wait_ge(x2_made, p + 1)
                for i in range(2):
                    nc.vector.bn_stats(stats2[:, 2 * p + i], x2[:, b, t + i]).then_inc(stat2_step, 1)
                dve.wait_ge(stat2_step, 4 * p + 2)
                for i in range(2):
                    nc.vector.bn_aggr(mean_var2[:, 2 * p + i], stats2[:, 2 * p + i]).then_inc(stat2_step, 1)
                dve.wait_ge(stat2_step, 4 * p + 4)

            def statistics2(b):
                nc.vector.tensor_scalar(var_eps2[:, b], mean_var2[:, b * T:(b + 1) * T, 1], LN_EPS, None,
                                        ALU.add).then_inc(ln2, 1)

            def normalise2(b):
                dve.wait_ge(pow2, b + 1)
                for t in range(T):
                    nc.vector.tensor_scalar(xn2[:, b * T + t], x2[:, b, t], mean_var2[:, b * T + t, 0:1],
                                            rstd2[:, b, t:t + 1], ALU.subtract, ALU.mult).then_inc(xn2_made, 1)

            def tokens2_rest(b):
                dve.wait_ge(xn2_hi_made, b + 1)
                nc.vector.tensor_tensor(xn2T_lo[:, b], bank[6][:], xn2T_hi[:, b].bitcast(F32),
                                        ALU.subtract).then_inc(xn2_lo_made, 1)

            def sum_logits(b):
                dve.wait_ge(logits_made, b + 1)
                nc.vector.tensor_reduce(logits[:, b * T:(b + 1) * T],
                                        logits_bank[b][:, 0:T * 2 * E].rearrange("p (t w e) -> p t e w", w=2, e=E),
                                        AX_X, ALU.add).then_inc(logits_out, 1)

            def top_values(b):
                dve.wait_ge(logits_out, b + 1)
                for t in range(T):
                    top = nc.vector.max(top8[:, b * T + t], logits[:, b * T + t])
                top.then_inc(top8_made, 1)

            def top_places(b):
                dve.wait_ge(top8_made, b + 1)
                for t in range(T):
                    at = nc.vector.max_index(top8_at[:, b * T + t], top8[:, b * T + t], logits[:, b * T + t])
                at.then_inc(top8_at_made, 1)

            def mark_chosen(b):
                dve.wait_ge(const_made, 3)
                dve.wait_ge(top8_at_made, b + 1)
                nc.vector.tensor_tensor(is_chosen[:, b].rearrange("p (t k) e -> p t k e", k=2),
                                        expert_no[:].unsqueeze(1).unsqueeze(1).broadcast_to([P, T, 2, E]),
                                        top8_at[:, b * T:(b + 1) * T, 0:2].unsqueeze(3).broadcast_to([P, T, 2, E]),
                                        ALU.is_equal).then_inc(chosen_made, 1)

            def gate_values(b):
                pair = "p (t k) -> p t k"
                sig = top2_sig[:, b, 0].rearrange(pair, k=2)
                dve.wait_ge(gate_exp_made, b + 1)
                nc.vector.tensor_scalar(top2_exp[:, b, 1], top2_exp[:, b, 0], 1.0, None, ALU.add).then_inc(gate_step, 1)
                yield
                dve.wait_ge(gate_step, 6 * b + 1)
                nc.vector.reciprocal(top2_sig[:, b, 0], top2_exp[:, b, 1]).then_inc(gate_step, 1)
                yield
                dve.wait_ge(gate_step, 6 * b + 2)
                nc.vector.scalar_tensor_tensor(out=gate_sum[:, b, 0], in0=sig[:, :, 0], scalar=GATE_EPS,
                                               in1=sig[:, :, 1], op0=ALU.add, op1=ALU.add).then_inc(gate_step, 1)
                yield
                dve.wait_ge(gate_step, 6 * b + 3)
                nc.vector.reciprocal(gate_sum[:, b, 1], gate_sum[:, b, 0]).then_inc(gate_step, 1)
                yield
                dve.wait_ge(gate_step, 6 * b + 4)
                nc.vector.tensor_tensor(top2_sig[:, b, 1].rearrange(pair, k=2), sig,
                                        gate_sum[:, b, 1].unsqueeze(2).broadcast_to([P, T, 2]), ALU.mult).then_inc(gate_step, 1)
                yield
                dve.wait_ge(gate_step, 6 * b + 5)
                dve.wait_ge(chosen_made, b + 1)
                nc.vector.tensor_tensor(chosen_gate[:, b], is_chosen[:, b],
                                        top2_sig[:, b, 1].unsqueeze(2).broadcast_to([P, 2 * T, E]), ALU.mult).then_inc(gate_step, 1)
                yield
                dve.wait_ge(gate_step, 6 * b + 6)
                both = chosen_gate[:, b].rearrange("p (t k) e -> p t k e", k=2)
                nc.vector.tensor_tensor(gates[:, b * T:(b + 1) * T], both[:, :, 0], both[:, :, 1], ALU.add).then_inc(gates_made, 1)
                yield

            def gatesT_copy(b):
                dve.wait_ge(gatesT_made, b + 1)
                nc.vector.tensor_copy(gatesT[:, b * S:(b + 1) * S], gatesT_bank[b][0:E, :]).then_inc(gatesT_out, 1)

            def hidden(n, first=0):
                dve.wait_ge(silu_done, first + (n + 1))
                dve.wait_ge(up_done, first + (n + 1))
                if n >= 2:
                    dve.wait_ge(hid_lo_done, first + (n - 1))
                nc.vector.tensor_tensor(hid[:, n % 2], up_bank[n % 2][:], silu_g[:, n % 2], ALU.mult).then_inc(hid_done, 1)

            def hidden_rest(n, first=0):
                dve.wait_ge(hid_hi_done, first + (n + 1))
                nc.vector.tensor_tensor(hid_lo[:, n % 4], hid[:, n % 2], hid_hi[:, n % 4].bitcast(F32),
                                        ALU.subtract).then_inc(hid_lo_done, 1)

            def weigh(q, j=0):
                dve.wait_ge(down_done, j * UNITS + (2 * q + 2))
                if q < PAIRS:
                    dve.wait_ge(gate_spread, q + 1)
                else:
                    dve.wait_ge(in_gate_row[q % PAIRS], (j + q // PAIRS) * 16)
                dve.wait_ge(acc_done, j * PAIRS + (q + 1))
                nc.vector.tensor_tensor(weighted[:, q % 2], down_bank[q % 2][:], gate_row[:, q % PAIRS],
                                        ALU.mult).then_inc(weighted_done, 1)

            def unit(n, j=0):
                hidden(n, j * UNITS)
                if n % 2 == 1 and n >= 5:
                    weigh((n - 5) // 2, j)
                hidden_rest(n, j * UNITS)

            shift(0)
            shift(1)
            sums(0)
            normalise(dve, 0)
            sums(1)
            normalise(dve, 1)
            exp_scale(1)
            shift(2)
            residual(0)
            residual(1)
            statistics2(0)
            shift(3)
            normalise2(0)
            split_router()
            sums(2)
            tokens2_rest(0)
            sums(3)

            first_gates = gate_values(0)
            second_gates = gate_values(1)
            hidden(0)
            sum_logits(0)
            hidden_rest(0)
            residual(2)
            hidden(1)
            residual(3)
            statistics2(1)
            hidden_rest(1)
            top_values(0)
            hidden(2)
            top_places(0)
            hidden_rest(2)
            mark_chosen(0)
            normalise2(1)
            hidden(3)
            next(first_gates)
            next(first_gates)
            next(first_gates)
            hidden_rest(3)
            next(first_gates)
            next(first_gates)
            next(first_gates)
            next(first_gates)
            tokens2_rest(1)
            hidden(4)
            hidden_rest(4)
            sum_logits(1)
            top_values(1)
            top_places(1)
            hidden(5)
            weigh(0)
            hidden_rest(5)
            mark_chosen(1)
            next(second_gates)
            next(second_gates)
            hidden(6)
            next(second_gates)
            next(second_gates)
            hidden_rest(6)
            next(second_gates)
            next(second_gates)
            gatesT_copy(0)
            hidden(7)
            next(second_gates)
            weigh(1)
            hidden_rest(7)
            hidden(8)
            hidden_rest(8)
            for n in range(9, HEADSTART):
                unit(n)
                if n == 10:
                    gatesT_copy(1)
            with dve.Fori(0, LOOPS) as j:
                for n in range(HEADSTART, HEADSTART + UNITS):
                    unit(n, j)
            for n in range(ROUNDS * UNITS - 3, ROUNDS * UNITS):
                unit(n)
            for q in range(ROUNDS * PAIRS - 2, ROUNDS * PAIRS):
                weigh(q)
            for b in range(B):
                dve.wait_ge(accT_made, b + 1)
                nc.vector.scalar_tensor_tensor(out=y[:, b], in0=bank[6 + b][:].rearrange("p (t d) -> p t d", t=T),
                                               scalar=g_tanh[:, 1:2], in1=x2[:, b], op0=ALU.mult, op1=ALU.add).then_inc(y_made, 1)

        @block.tensor
        def _(pe):
            def keep_warm(times, free_bank):
                for _ in range(times):
                    nc.tensor.matmul(free_bank[:], blank[:, 0:P], blank[:], start=True, stop=True)

            pe.wait_ge(blank_made, 1)
            keep_warm(WARM0, bank[0])
            pe.wait_ge(ident_made, 1)
            pe.wait_ge(in_ctx, 16)
            nc.tensor.transpose(bank[7][:, 0:B * M], ctx_sb[:], ident[0:B * M, 0:B * M]).then_inc(ctxT_made, 1)

            def project_ctx(w, w_in, bk, made):
                pe.wait_ge(w_in, 16)
                for c in range(HC):
                    mm = nc.tensor.matmul(bk[:, c * B * M:(c + 1) * B * M], w[:, c * P:(c + 1) * P], ctxT[:],
                                          start=True, stop=True)
                mm.then_inc(made, 1)

            def turn_tokens(b):
                pe.wait_ge(in_x[b], 16)
                for t in range(T):
                    mm = nc.tensor.transpose(bank[2 + b][:, t * P:(t + 1) * P], x_sb[:, b, t], ident[:])
                mm.then_inc(xT_made, 1)

            pe.wait_ge(ctxT_out, 1)
            project_ctx(wk_sb, in_wk, bank[5], k_made)
            pe.wait_ge(center_made, 1)
            pe.wait_ge(in_wq, 16)
            for c in range(HC):
                mm = nc.tensor.matmul(bank[6][:, c * D:(c + 1) * D], wq_sb[:, c * P:(c + 1) * P], center[:],
                                      start=True, stop=True)
            mm.then_inc(wqT_made, 1)
            turn_tokens(0)
            pe.wait_ge(wqT_out, 1)
            pe.wait_ge(k_out, 2)
            for c in range(HC):
                mm = nc.tensor.matmul(bank[4][:, c * P:(c + 1) * P], wqT[:, c], k_diag[:, c].rearrange("p r k -> p (r k)"),
                                      start=True, stop=True)
            mm.then_inc(m_made, 1)
            project_ctx(wv_sb, in_wv, bank[7], v_made)
            turn_tokens(1)

            def fold_out():
                pe.wait_ge(v_out, 4)
                pe.wait_ge(in_wo, 16)
                for b in range(B):
                    for g in range(2):
                        for k in range(2):
                            mm = nc.tensor.matmul(bank[5][:, (2 * b + g) * D:(2 * b + g + 1) * D], v_diag[:, b, g, k],
                                                  wo_sb[:, 2 * g + k], start=(k == 0), stop=(k == 1))
                mm.then_inc(u_made, 1)

            def scores(p):
                b = p // 2
                pe.wait_ge(xT_out, b + 1)
                pe.wait_ge(m_out, 1)
                if p >= 2:
                    pe.wait_ge(shift_made, p - 1)
                for t in range(2):
                    mm = nc.tensor.matmul(bank[p % 2][:, t * HM:(t + 1) * HM], xT[:, 2 * p + t],
                                          m_sb[:, b].rearrange("p h m -> p (h m)"), start=True, stop=True)
                mm.then_inc(scores_made, 1)

            def turn_probs(p):
                pe.wait_ge(probs_made[p], 1)
                if p < 2:
                    pe.wait_ge(xT_out, p + 1)
                if p == 2:
                    pe.wait_ge(xn2_lo_made, 1)
                for t in range(2):
                    for g in range(2):
                        at = (2 * t + g) * P
                        mm = nc.tensor.transpose(probsT_bank[p][:, at:at + P], probs[:, p % 2, t, g * P:(g + 1) * P], ident[:])
                mm.then_inc(probsT_made, 1)

            def attention(p):
                b = p // 2
                pe.wait_ge(probsT_out, p + 1)
                pe.wait_ge(u_out, 1)
                for t in range(2):
                    for g in range(2):
                        mm = nc.tensor.matmul(attn_bank[p][:, t * D:(t + 1) * D], probsT[:, p % 2, t, g],
                                              u_sb[:, b, g], start=(g == 0), stop=(g == 1))
                mm.then_inc(attn_made, 1)

            def turn_tokens2(b):
                for t in range(T):
                    pe.wait_ge(xn2_made, T * b + t + 1)
                    mm = nc.tensor.transpose(bank[6][:, t * P:(t + 1) * P], xn2[:, b * T + t], ident[:])
                mm.then_inc(xn2T_made, 1)

            def route(b):
                pe.wait_ge(rwT_out, 3)
                pe.wait_ge(xn2_lo_made, b + 1)
                pe.wait_ge(x2_made, 2 * b + 2)
                for t in range(T):
                    for i, xt in enumerate((xn2T_hi, xn2T_lo)):
                        mm = nc.tensor.matmul(logits_bank[b][:, t * 2 * E:(t + 1) * 2 * E], xt[:, b, t * P:(t + 1) * P],
                                              rwT_parts[:].rearrange("p w e -> p (w e)"), start=(i == 0), stop=(i == 1))
                mm.then_inc(logits_made, 1)

            def spread_gates(b, k):
                pe.wait_ge(gates_made, b + 1)
                if (b, k) != (0, 0):
                    pe.wait_ge(gate_spread, b * EP + k)
                for t in range(T):
                    mm = nc.tensor.transpose(spread_bank[b][:, t * P:(t + 1) * P],
                                             gates[:, b * T + t, k:k + 1].broadcast_to([P, P]), ident[:])
                mm.then_inc(spread_made, 1)

            def turn_gates(b):
                pe.wait_ge(gates_made, b + 1)
                if b == 0:
                    pe.wait_ge(logits_out, 2)
                else:
                    pe.wait_ge(gatesT_out, 1)
                for t in range(T):
                    mm = nc.tensor.transpose(gatesT_bank[b][0:E, t * P:(t + 1) * P], gates[:, b * T + t], ident[:])
                mm.then_inc(gatesT_made, 1)

            scores(0)
            scores(1)
            fold_out()
            keep_warm(WARM1, bank[7])
            pe.wait_ge(in_rw, 16)
            nc.tensor.transpose(bank[6][:, 0:E], rw_sb[:], ident[0:E, 0:E]).then_inc(rwT_made, 1)
            scores(2)
            scores(3)
            turn_probs(0)
            keep_warm(WARM2, bank[7])
            attention(0)
            turn_probs(1)
            keep_warm(WARM3, bank[7])
            attention(1)
            keep_warm(WARM5, bank[7])
            pe.wait_ge(rwT_out, 1)
            turn_tokens2(0)
            keep_warm(WARM4, bank[7])

            def gate_up(n, j=0, first_of_half=False):
                half, k, c = unit_of(n)
                cols = slice(c * P, (c + 1) * P)
                dest = ((gate_bank[n % 2], gate_done), (up_bank[n % 2], up_done))

                def product(i, w, xt, start=False, stop=False):
                    mm = nc.tensor.matmul(dest[i][0][:], w[:, k, i, cols], xt[:, half], start=start, stop=stop)
                    if stop:
                        mm.then_inc(dest[i][1], 1)

                pe.wait_ge(w_lo_done, (j + n // UNITS) * 4 + (k + 1))
                if n >= 2:
                    pe.wait_ge(hid_done, j * UNITS + (n - 1))
                if first_of_half:
                    pe.wait_ge(xn2_hi_made, half + 1)
                    for i in range(2):
                        product(i, gu_hi, xn2T_hi, start=True)
                        product(i, gu_lo, xn2T_hi)
                    pe.wait_ge(xn2_lo_made, half + 1)
                    for i in range(2):
                        product(i, gu_hi, xn2T_lo, stop=True)
                else:
                    for i in range(2):
                        product(i, gu_hi, xn2T_hi, start=True)
                        product(i, gu_lo, xn2T_hi)
                        product(i, gu_hi, xn2T_lo, stop=True)

            def down(n, j=0):
                half, k, c = unit_of(n)
                q = n // FC
                pe.wait_ge(hid_lo_done, j * UNITS + (n + 1))
                pe.wait_ge(w_lo_done, (j + n // UNITS) * 4 + (k + 3))
                if c == 0 and q >= 2:
                    pe.wait_ge(weighted_done, j * PAIRS + (q - 1))
                terms = [(d_hi, hid_hi), (d_lo, hid_hi), (d_hi, hid_lo)]
                for s, (w, h) in enumerate(terms):
                    mm = nc.tensor.matmul(down_bank[q % 2][:], w[:, k, c], h[:, n % 4],
                                          start=(c == 0 and s == 0), stop=(c == FC - 1 and s == len(terms) - 1))
                mm.then_inc(down_done, 1)

            pe.wait_ge(shift_made, 4)
            pe.wait_ge(probsT_out, 2)
            gate_up(0, first_of_half=True)
            turn_probs(2)
            route(0)
            gate_up(1)
            attention(2)
            turn_probs(3)
            keep_warm(WARM5, bank[4])
            attention(3)
            gate_up(2)
            down(0)
            gate_up(3)
            down(1)
            pe.wait_ge(x2_made, 3)
            turn_tokens2(1)
            gate_up(4, first_of_half=True)
            pe.wait_ge(logits_out, 1)
            down(2)
            route(1)
            for n in range(5, HEADSTART):
                if n in SPREAD_AT:
                    q = SPREAD_AT.index(n)
                    spread_gates(q // EP, q % EP)
                gate_up(n)
                down(n - LAG)
                if n in TURN_AT:
                    turn_gates(TURN_AT.index(n))
            with pe.Fori(0, LOOPS) as j:
                for n in range(HEADSTART, HEADSTART + UNITS):
                    gate_up(n, j)
                    down(n - LAG, j)
            for n in range(ROUNDS * UNITS - 3, ROUNDS * UNITS):
                gate_up(n)
                down(n - LAG)
            for n in range(ROUNDS * UNITS - LAG, ROUNDS * UNITS):
                down(n)
            for b in range(B):
                pe.wait_ge(acc_done, B + ROUNDS * PAIRS - EP * (B - 1 - b))
                for t in range(T):
                    mm = nc.tensor.transpose(bank[6 + b][:, t * P:(t + 1) * P], acc[:, b, t * P:(t + 1) * P], ident[:])
                mm.then_inc(accT_made, 1)


_INS = ['x', 'ctx_1024', 'g_xattn', 'g_ffn', 'L0_xattn_Wq', 'L0_xattn_Wk', 'L0_xattn_Wv', 'L0_xattn_Wo',
        'L0_xattn_bo', 'L0_ffn_router_w', 'L0_ffn_w_gate', 'L0_ffn_w_up', 'L0_ffn_w_down']
_OUTS = [((2, 512, 128), 'float32')]


def kernel(**inputs):
    import numpy as _np
    import concourse.bacc as _bacc
    from concourse import mybir as _mybir
    from concourse.bass_utils import run_bass_kernel_spmd as _run

    nc = _bacc.Bacc("TRN2", target_bir_lowering=False, num_devices=1)
    arrays, args = {}, []
    for name in _INS:
        a = _np.ascontiguousarray(inputs[name])
        arrays[f"in_{name}_dram"] = a
        args.append(nc.dram_tensor(f"in_{name}_dram", a.shape, _mybir.dt.from_np(a.dtype), kind="ExternalInput").ap())
    for i, (shape, dtype) in enumerate(_OUTS):
        dt = _mybir.dt.from_np(_np.dtype(dtype))
        args.append(nc.dram_tensor(f"out_{i}_dram", shape, dt, kind="ExternalOutput").ap())
    gated_cross_attention_and_top2_experts(nc, *args)
    r = _run(nc, [arrays], core_ids=[0])
    got = tuple(r.results[0][f"out_{i}_dram"] for i in range(len(_OUTS)))
    return got[0]
```

```python
import math
from contextlib import ExitStack

import concourse.bass as bass
from concourse import mybir

P = 128
F32 = mybir.dt.float32
F32R = mybir.dt.float32r
BF16 = mybir.dt.bfloat16
U32 = mybir.dt.uint32
ALU = mybir.AluOpType
ACT = mybir.ActivationFunctionType
AX_X = mybir.AxisListType.X


def gated_cross_attention_and_top2_experts(
    nc: bass.Bass,
    x: bass.AP,
    ctx: bass.AP,
    g_xattn: bass.AP,
    g_ffn: bass.AP,
    Wq: bass.AP,
    Wk: bass.AP,
    Wv: bass.AP,
    Wo: bass.AP,
    bo: bass.AP,
    router_w: bass.AP,
    w_gate: bass.AP,
    w_up: bass.AP,
    w_down: bass.AP,
    out: bass.AP,
):
    B, S, D = x.shape
    M = ctx.shape[1]
    HID = Wq.shape[1]
    DH = 64
    HEADS = HID // DH
    E, _, H = w_gate.shape
    T = S // P
    NT = B * T
    HC = HID // P
    HM = HEADS * M
    FC = H // P
    SCALE = DH ** -0.5
    LN_EPS = 1e-5
    GATE_EPS = 1e-10
    assert D == P and B == 2 and S == 512 and HM == 256 and E == 8 and FC == 2

    EP = 2
    ROUNDS = E // EP
    UNITS = EP * B * FC
    PAIRS = EP * B
    N, Q = ROUNDS * UNITS, ROUNDS * PAIRS
    LAG = 2
    HEADSTART = 13

    WARM_INPUTS, WARM_CTX, WARM_NORM = 8, 2, 13
    SPREAD_AT = (5, 6, 9, 10)
    TURN_AT = (6, 9)
    RESTS_BEHIND = 11
    LOOPS = ROUNDS - 2
    x_rows = x.rearrange("b (p t) d -> p b t d", t=T)
    out_rows = out.rearrange("b (p t) d -> p b t d", t=T)
    ctx_rows = ctx.rearrange("b m d -> (b m) d")
    Wo_rows = Wo.rearrange("(c k) n -> k c n", k=P)

    with ExitStack() as stack:
        def sb(name, shape, dt=F32):
            return stack.enter_context(nc.sbuf_tensor(name, shape, dt))

        def sem(name):
            return stack.enter_context(nc.semaphore(name))

        bank = [stack.enter_context(nc.psum_tensor(f"bank{i}", [P, 512], F32)) for i in range(8)]
        gates_dram = nc.dram_tensor("gates_dram", [E, B * S], F32, kind="Internal").ap()

        ident = sb("ident", [P, P])
        blank = sb("blank", [P, P], BF16)
        center = sb("center", [P, P])
        expert_no = sb("expert_no", [P, E])
        minus_half = sb("minus_half", [P, T])
        inv_e = sb("inv_e", [P, 2 * T])
        x_sb = sb("x_sb", [P, B, T, D])
        ctx_sb = sb("ctx_sb", [B * M, D])
        wq_sb = sb("wq_sb", [P, HID])
        wk_sb = sb("wk_sb", [P, HID])
        wv_sb = sb("wv_sb", [P, HID])
        wo_sb = sb("wo_sb", [P, HC, D])
        bo_sb = sb("bo_sb", [P, D])
        rw_sb = sb("rw_sb", [E, D])
        g_raw = sb("g_raw", [P, 2])
        g_tanh = sb("g_tanh", [P, 2])
        ctxT = sb("ctxT", [P, B * M])
        rwT = sb("rwT", [P, E])
        rwT_parts = sb("rwT_parts", [P, 2, E], F32R)
        wqT = sb("wqT", [P, HC, D])
        k_diag = sb("k_diag", [P, HC, 2, B * M])
        v_diag = sb("v_diag", [P, B, 2, 2, P])
        m_sb = sb("m_sb", [P, B, HEADS, M])
        u_sb = sb("u_sb", [P, B, 2, D])
        xT = sb("xT", [P, NT, P])
        stats = sb("stats", [P, NT, 6])
        mean_var = sb("mean_var", [P, NT, 2])
        var_eps = sb("var_eps", [P, B, T])
        rstd = sb("rstd", [P, B, T])
        rstd_scale = sb("rstd_scale", [P, NT])
        x_bias = sb("x_bias", [P, B, T, D])
        row_max = sb("row_max", [P, 2, 2 * HEADS])
        shifted = sb("shifted", [P, 2, 2, HM])
        expd = sb("expd", [P, 2, 2, HM])
        row_sum = sb("row_sum", [P, 2, 2 * HEADS])
        row_inv = sb("row_inv", [P, 2, 2 * HEADS])
        probs = sb("probs", [P, 2, 2, HM])
        probsT = sb("probsT", [P, 2, 2, 2, P])
        x2 = sb("x2", [P, B, T, D])
        stats2 = sb("stats2", [P, NT, 6])
        mean_var2 = sb("mean_var2", [P, NT, 2])
        var_eps2 = sb("var_eps2", [P, B, T])
        rstd2 = sb("rstd2", [P, B, T])
        xn2 = sb("xn2", [P, NT, D])
        xn2T_hi = sb("xn2T_hi", [P, B, S], F32R)
        xn2T_lo = sb("xn2T_lo", [P, B, S], F32R)
        logits = sb("logits", [P, NT, E])
        top8 = sb("top8", [P, NT, 8])
        top8_at = sb("top8_at", [P, NT, 8], U32)
        top2_exp = sb("top2_exp", [P, B, 2, 2 * T])
        top2_sig = sb("top2_sig", [P, B, 2, 2 * T])
        gate_sum = sb("gate_sum", [P, B, 3, T])
        is_chosen = sb("is_chosen", [P, B, 2 * T, E])
        chosen_gate = sb("chosen_gate", [P, B, 2 * T, E])
        gates = sb("gates", [P, NT, E])
        gatesT = sb("gatesT", [E, B * S])
        raw_gu = sb("raw_gu", [P, EP, 2, H])
        raw_d = sb("raw_d", [P, EP, FC, D])
        gu_hi = sb("gu_hi", [P, EP, 2, H], F32R)
        gu_lo = sb("gu_lo", [P, EP, 2, H], F32R)
        d_hi = sb("d_hi", [P, EP, FC, D], F32R)
        d_lo = sb("d_lo", [P, EP, FC, D], F32R)
        silu_g = sb("silu_g", [P, 2, S])
        hid = sb("hid", [P, 2, S])
        hid_hi = sb("hid_hi", [P, 4, S], F32R)
        hid_lo = sb("hid_lo", [P, 4, S], F32R)
        gate_row = sb("gate_row", [P, PAIRS, S])
        weighted = sb("weighted", [P, 2, S])
        acc = sb("acc", [P, B, S])
        y = sb("y", [P, B, T, D])

        in_x = [sem(f"in_x{b}") for b in range(B)]
        in_ctx, in_wq, in_wk, in_wv, in_wo = (sem(f"in_{n}") for n in ("ctx", "wq", "wk", "wv", "wo"))
        in_bo, in_rw, in_g = sem("in_bo"), sem("in_rw"), sem("in_g")
        in_gu = [sem(f"in_gu{i}") for i in range(EP)]
        in_d = [sem(f"in_d{i}") for i in range(EP)]
        in_gate_row = [sem(f"in_gate_row{i}") for i in range(PAIRS)]
        gates_stored = [sem(f"gates_stored{b}") for b in range(B)]
        out_stored = [sem(f"out_stored{b}") for b in range(B)]
        zeroed, blank_made = sem("zeroed"), sem("blank_made")
        ident_made, center_made = sem("ident_made"), sem("center_made")
        k_zeroed, v_zeroed = sem("k_zeroed"), sem("v_zeroed")
        const_made = sem("const_made")
        ctxT_made, ctxT_out = sem("ctxT_made"), sem("ctxT_out")
        rwT_made, rwT_out = sem("rwT_made"), sem("rwT_out")
        wqT_made, wqT_out = sem("wqT_made"), sem("wqT_out")
        k_made, v_made, k_out, v_out = sem("k_made"), sem("v_made"), sem("k_out"), sem("v_out")
        m_made, m_out, u_made, u_out = sem("m_made"), sem("m_out"), sem("u_made"), sem("u_out")
        xT_made, xT_out = sem("xT_made"), sem("xT_out")
        tanh_made = sem("tanh_made")
        bo_scaled, bias_made = sem("bo_scaled"), sem("bias_made")
        stat1_step, var1_made, pow1, scale1_made = (
            sem("stat1_step"), sem("var1_made"), sem("pow1"), sem("scale1_made"))
        scores_made, shift_made, exp_made = sem("scores_made"), sem("shift_made"), sem("exp_made")
        max_made, stat2_step = sem("max_made"), sem("stat2_step")
        sum_made, inv_made = sem("sum_made"), sem("inv_made")
        probs_made = [sem(f"probs_made{p}") for p in range(NT // 2)]
        probsT_made, probsT_out = sem("probsT_made"), sem("probsT_out")
        attn_made, x2_made = sem("attn_made"), sem("x2_made")
        ln2, pow2, xn2_made = sem("ln2"), sem("pow2"), sem("xn2_made")
        xn2T_made, xn2_hi_made, xn2_lo_made = sem("xn2T_made"), sem("xn2_hi_made"), sem("xn2_lo_made")
        logits_made, logits_out = sem("logits_made"), sem("logits_out")
        top8_made, top8_at_made, chosen_made, gate_step, gates_made = (
            sem("top8_made"), sem("top8_at_made"), sem("chosen_made"), sem("gate_step"), sem("gates_made"))
        gate_exp_made = sem("gate_exp_made")
        spread_made, gate_spread = sem("spread_made"), sem("gate_spread")
        gatesT_made, gatesT_out = sem("gatesT_made"), sem("gatesT_out")
        w_hi_done, w_lo_done = sem("w_hi_done"), sem("w_lo_done")
        gate_done, up_done, down_done = sem("gate_done"), sem("up_done"), sem("down_done")
        silu_done, hid_done, hid_hi_done, hid_lo_done = (
            sem("silu_done"), sem("hid_done"), sem("hid_hi_done"), sem("hid_lo_done"))
        weighted_done, acc_done = sem("weighted_done"), sem("acc_done")
        accT_made, y_made = sem("accT_made"), sem("y_made")

        gate_bank, up_bank, down_bank = bank[0:2], bank[2:4], bank[4:6]
        probsT_bank = [bank[2], bank[3], bank[5], bank[4]]
        attn_bank = [bank[4], bank[5], bank[7], bank[5]]
        logits_bank = [bank[6], bank[7]]
        gatesT_bank, spread_bank = bank[7], bank[6]
        sum_bank = [bank[6], bank[7], bank[0]]

        def unit_of(n):
            m = n % UNITS
            return m // (EP * FC), (m // FC) % EP, m % FC

        def normalise(eng, p):
            eng.wait_ge(exp_made, 2 * p + 2)
            eng.wait_ge(inv_made, p + 1)
            if p >= 2:
                eng.wait_ge(probsT_made, p - 1)
            eng.tensor_tensor(
                probs[:, p % 2].rearrange("p t (h m) -> p (t h) m", m=M),
                expd[:, p % 2].rearrange("p t (h m) -> p (t h) m", m=M),
                row_inv[:, p % 2].unsqueeze(2).broadcast_to([P, 2 * HEADS, M]), ALU.mult).then_inc(probs_made[p], 1)

        block = stack.enter_context(nc.Block())

        @block.sync
        def _(sp):
            sp.dma_start(ctx_sb[:], ctx_rows).then_inc(in_ctx, 16)
            sp.dma_start(wq_sb[:], Wq).then_inc(in_wq, 16)
            sp.dma_start(g_raw[:, 0:1], g_xattn.rearrange("(a n) -> a n", a=1).broadcast_to([P, 1])).then_inc(in_g, 16)
            sp.dma_start(g_raw[:, 1:2], g_ffn.rearrange("(a n) -> a n", a=1).broadcast_to([P, 1])).then_inc(in_g, 16)
            sp.dma_start(wv_sb[:], Wv).then_inc(in_wv, 16)
            sp.dma_start(rw_sb[:], router_w).then_inc(in_rw, 16)
            sp.dma_start(bo_sb[:], bo.rearrange("(a n) -> a n", a=1).broadcast_to([P, D])).then_inc(in_bo, 16)
            sp.dma_start(wo_sb[:], Wo_rows).then_inc(in_wo, 16)

            def load_gate_up(e, k):
                for i, w in enumerate((w_gate, w_up)):
                    sp.dma_start(raw_gu[:, k, i], w[bass.ds(e, 1)].rearrange("a d h -> (a d) h")).then_inc(in_gu[k], 16)

            def load_down(e, k):
                sp.dma_start(raw_d[:, k], w_down[bass.ds(e, 1)].rearrange("a (c p) d -> (a p) c d", p=P)
                             ).then_inc(in_d[k], 16)

            for k in range(EP):
                load_gate_up(k, k)
            for k in range(EP):
                load_down(k, k)

            def load_gate_row(e, q):
                half, k = q // EP, q % EP
                src = gates_dram[bass.ds(e, 1), half * S:(half + 1) * S]
                sp.dma_start(gate_row[:, q], src.broadcast_to([P, S])).then_inc(in_gate_row[q], 16)

            def pass_gates(b):
                sp.wait_ge(gatesT_out, b + 1)
                sp.dma_start(gates_dram[:, b * S:(b + 1) * S], gatesT[:, b * S:(b + 1) * S]
                             ).then_inc(gates_stored[b], 16)

            def next_weights(i, r):
                sp.wait_ge(w_lo_done, r * 4 + (i + 1))
                load = load_gate_up if i < EP else load_down
                load(r * EP + (EP + i % EP), i % EP)

            def next_gate_row(q, r):
                sp.wait_ge(weighted_done, r * PAIRS + (q + 1))
                load_gate_row(r * EP + (EP + q % EP), q)

            for q in range(PAIRS):
                next_weights(q, 0)
            pass_gates(0)
            sp.wait_ge(gates_stored[0], 16)
            next_gate_row(0, 0)
            next_gate_row(1, 0)
            pass_gates(1)
            sp.wait_ge(gates_stored[1], 16)
            with sp.Fori(0, LOOPS) as j:
                next_weights(0, j + 1)
                next_weights(1, j + 1)
                next_gate_row(2, j)
                next_gate_row(3, j)
                next_weights(2, j + 1)
                next_weights(3, j + 1)
                next_gate_row(0, j + 1)
                next_gate_row(1, j + 1)
            next_gate_row(2, LOOPS)
            next_gate_row(3, LOOPS)
            sp.wait_ge(y_made, 1)
            sp.dma_start(out_rows[:, 0], y[:, 0]).then_inc(out_stored[0], 16)
            sp.wait_ge(y_made, 2)
            sp.dma_start(out_rows[:, 1, 0:2], y[:, 1, 0:2]).then_inc(out_stored[1], 16)
            sp.wait_ge(out_stored[0], 16)
            sp.wait_ge(out_stored[1], 32)

        @block.gpsimd
        def _(pool):
            nc.gpsimd.memset(ident[:], 0.0).then_inc(zeroed, 1)
            pool.wait_ge(zeroed, 1)
            nc.gpsimd.affine_select(out=ident[:], in_=ident[:], compare_op=ALU.not_equal, fill=1.0, base=0,
                                    pattern=[[-1, P]], channel_multiplier=1).then_inc(ident_made, 1)
            nc.gpsimd.memset(center[:], -1.0 / D).then_inc(zeroed, 1)
            pool.wait_ge(zeroed, 2)
            nc.gpsimd.affine_select(out=center[:], in_=center[:], compare_op=ALU.not_equal, fill=1.0 - 1.0 / D,
                                    base=0, pattern=[[-1, P]], channel_multiplier=1).then_inc(center_made, 1)
            nc.gpsimd.memset(k_diag[:], 0.0).then_inc(k_zeroed, 1)
            nc.gpsimd.memset(v_diag[:], 0.0).then_inc(v_zeroed, 1)
            nc.gpsimd.memset(minus_half[:], -0.5).then_inc(const_made, 1)
            nc.gpsimd.memset(inv_e[:], math.exp(-1.0)).then_inc(const_made, 1)
            nc.gpsimd.iota(expert_no[:], pattern=[[1, E]], base=0, channel_multiplier=0,
                           allow_small_or_imprecise_dtypes=True).then_inc(const_made, 1)

            def split_rest(raw, hi, lo, raw_in, raw_value, hi_value, free=None):
                pool.wait_ge(raw_in, raw_value)
                pool.wait_ge(w_hi_done, hi_value)
                if free:
                    pool.wait_ge(*free)
                nc.gpsimd.tensor_tensor(lo, raw, hi.bitcast(F32), ALU.subtract).then_inc(w_lo_done, 1)

            def rest_gate_up(k, i, free=None):
                split_rest(raw_gu[:, k], gu_hi[:, k], gu_lo[:, k], in_gu[k], (i + 1) * 32, i * 4 + (k + 1), free)

            def rest_down(k, i, free=None):
                split_rest(raw_d[:, k], d_hi[:, k], d_lo[:, k], in_d[k], (i + 1) * 16, i * 4 + (k + 3), free)

            def inv_std(b):
                pool.wait_ge(var1_made, b + 1)
                pool.wait_ge(const_made, 1)
                nc.gpsimd.tensor_tensor(rstd[:, b], var_eps[:, b], minus_half[:], ALU.pow).then_inc(pow1, 1)

            def add_bias(b):
                pool.wait_ge(bo_scaled, 1)
                pool.wait_ge(in_x[b], 16)
                nc.gpsimd.tensor_tensor(x_bias[:, b], x_sb[:, b],
                                        bo_sb[:].unsqueeze(1).broadcast_to([P, T, D]), ALU.add).then_inc(bias_made, 1)

            def inv_std2(b):
                pool.wait_ge(ln2, b + 1)
                nc.gpsimd.tensor_tensor(rstd2[:, b], var_eps2[:, b], minus_half[:], ALU.pow).then_inc(pow2, 1)

            def gate_exp(b):
                pool.wait_ge(const_made, 2)
                pool.wait_ge(top8_made, b + 1)
                nc.gpsimd.tensor_tensor(top2_exp[:, b, 0].rearrange("p (t k) -> p t k", k=2),
                                        inv_e[:].rearrange("p (t k) -> p t k", k=2),
                                        top8[:, b * T:(b + 1) * T, 0:2], ALU.pow).then_inc(gate_exp_made, 1)

            def add_pair(q, first=0):
                half = (q // EP) % B
                pool.wait_ge(weighted_done, first + (q + 1))
                pool.wait_ge(acc_done, first + (q + 2))
                nc.gpsimd.tensor_tensor(acc[:, half], acc[:, half], weighted[:, q % 2], ALU.add).then_inc(acc_done, 1)

            def unit(n, j):
                turn, m = n // UNITS, n % UNITS
                if m == 5:
                    rest_gate_up(0, j + (turn + 1), (up_done, j * UNITS + (n + 1)))
                if m == 7:
                    rest_gate_up(1, j + (turn + 1), (up_done, j * UNITS + (n + 1)))
                if m == 0:
                    rest_down(0, j + turn, (down_done, j * UNITS + (n - LAG)))
                if m == 2:
                    rest_down(1, j + turn, (down_done, j * UNITS + (n - LAG)))
                if n % 2 == 0:
                    add_pair((n - 4) // 2, j * PAIRS)

            inv_std(0)
            inv_std(1)
            add_bias(0)
            rest_gate_up(0, 0)
            add_bias(1)
            rest_gate_up(1, 0)
            inv_std2(0)
            normalise(pool, 2)
            rest_down(0, 0)
            rest_down(1, 0)
            normalise(pool, 3)
            gate_exp(0)
            inv_std2(1)
            for b in range(B):
                nc.gpsimd.memset(acc[:, b], 0.0).then_inc(acc_done, 1)
            unit(5, 0)
            gate_exp(1)
            unit(4, 0)
            for n in range(6, HEADSTART):
                unit(n, 0)
            with pool.Fori(0, LOOPS) as j:
                for n in range(HEADSTART, HEADSTART + UNITS):
                    unit(n, j)
            add_pair(Q - 3)

        @block.scalar
        def _(act):
            act.dma_start(wk_sb[:], Wk).then_inc(in_wk, 16)
            act.dma_start(x_sb[:, 0], x_rows[:, 0]).then_inc(in_x[0], 16)
            act.dma_start(x_sb[:, 1], x_rows[:, 1]).then_inc(in_x[1], 16)
            nc.scalar.preload_act_table(ACT.Exp)

            act.wait_ge(in_g, 32)
            nc.scalar.activation(g_tanh[:], g_raw[:], ACT.Tanh).then_inc(tanh_made, 1)
            act.wait_ge(wqT_made, 1)
            nc.scalar.activation(wqT[:], bank[6][:], ACT.Copy).then_inc(wqT_out, 1)
            act.wait_ge(xT_made, 1)
            nc.scalar.activation(xT[:, 0:T], bank[2][:], ACT.Copy).then_inc(xT_out, 1)
            act.wait_ge(m_made, 1)
            nc.scalar.activation(m_sb[:].rearrange("p b h m -> p h b m"),
                                 bank[4][:].rearrange("p (h b m) -> p h b m", b=B, m=M), ACT.Copy).then_inc(m_out, 1)
            act.wait_ge(xT_made, 2)
            nc.scalar.activation(xT[:, T:NT], bank[3][:], ACT.Copy).then_inc(xT_out, 1)

            def round_gate_up(k, i, free=None):
                act.wait_ge(in_gu[k], (i + 1) * 32)
                if free:
                    act.wait_ge(*free)
                nc.scalar.activation(gu_hi[:, k], raw_gu[:, k], ACT.Copy).then_inc(w_hi_done, 1)

            def round_down(k, i, free=None):
                act.wait_ge(in_d[k], (i + 1) * 16)
                if free:
                    act.wait_ge(*free)
                nc.scalar.activation(d_hi[:, k], raw_d[:, k], ACT.Copy).then_inc(w_hi_done, 1)

            def exponentials(p):
                act.wait_ge(shift_made, p + 1)
                act.wait_ge(scale1_made, p // 2 + 1)
                if p >= 2:
                    act.wait_ge(probs_made[p - 2], 1)
                for t in range(2):
                    nc.scalar.activation(expd[:, p % 2, t], shifted[:, p % 2, t], ACT.Exp,
                                         scale=rstd_scale[:, 2 * p + t:2 * p + t + 1]).then_inc(exp_made, 1)

            def probsT_copy(p):
                act.wait_ge(probsT_made, p + 1)
                if p >= 2:
                    act.wait_ge(attn_made, p - 1)
                nc.scalar.activation(probsT[:, p % 2], probsT_bank[p][:], ACT.Copy).then_inc(probsT_out, 1)

            def tokens2_round(b):
                act.wait_ge(xn2T_made, b + 1)
                nc.scalar.activation(xn2T_hi[:, b], bank[6][:], ACT.Copy).then_inc(xn2_hi_made, 1)

            exponentials(0)
            act.wait_ge(v_zeroed, 1)
            act.wait_ge(v_made, 1)
            for r in range(2):
                rows = slice(DH * r, DH * r + DH)
                v = bank[7][rows, 0:HC * B * M].rearrange("p (j k b m) -> p j k b m", j=2, k=2, b=B)
                for k in range(2):
                    h4 = 2 * k + r
                    nc.scalar.activation(v_diag[rows, :, :, k, h4 * M:(h4 + 1) * M],
                                         v[:, :, k].rearrange("p j b m -> p b j m"), ACT.Copy).then_inc(v_out, 1)
            exponentials(1)
            round_gate_up(0, 0)
            round_gate_up(1, 0)
            act.wait_ge(u_made, 1)
            nc.scalar.activation(u_sb[:], bank[5][:], ACT.Copy).then_inc(u_out, 1)
            probsT_copy(0)
            probsT_copy(1)
            exponentials(2)
            round_down(0, 0)
            round_down(1, 0)
            tokens2_round(0)
            probsT_copy(2)
            exponentials(3)
            nc.scalar.preload_act_table(ACT.Silu)

            def silu(n, first=0):
                act.wait_ge(gate_done, first + (n + 1))
                if n >= 2:
                    act.wait_ge(hid_done, first + (n - 1))
                nc.scalar.activation(silu_g[:, n % 2], gate_bank[n % 2][:], ACT.Silu).then_inc(silu_done, 1)

            def hid_round(n, first=0):
                act.wait_ge(hid_done, first + (n + 1))
                if n >= 4:
                    act.wait_ge(down_done, first + (n - 3))
                nc.scalar.activation(hid_hi[:, n % 4], hid[:, n % 2], ACT.Copy).then_inc(hid_hi_done, 1)

            def next_round(n, j):
                turn, m = n // UNITS, n % UNITS
                if m == 5:
                    round_gate_up(0, j + (turn + 1), (up_done, j * UNITS + (n + 1)))
                if m == 7:
                    round_gate_up(1, j + (turn + 1), (up_done, j * UNITS + (n + 1)))
                if m == 0 and n > 0:
                    round_down(0, j + turn, (down_done, j * UNITS + (n - LAG)))
                if m == 2 and n > 2:
                    round_down(1, j + turn, (down_done, j * UNITS + (n - LAG)))

            def unit(n, j=0):
                silu(n, j * UNITS)
                if n > RESTS_BEHIND:
                    hid_round(n - 1, j * UNITS)
                if n in SPREAD_AT:
                    spread_copy(SPREAD_AT.index(n))
                if n < N - 3:
                    next_round(n, j)
                if n == 3:
                    tokens2_round(1)
                if n < RESTS_BEHIND:
                    hid_round(n, j * UNITS)

            def spread_copy(q):
                act.wait_ge(spread_made, q + 1)
                nc.scalar.activation(gate_row[:, q], spread_bank[:], ACT.Copy).then_inc(gate_spread, 1)

            silu(0)
            probsT_copy(3)
            hid_round(0)
            for n in range(1, HEADSTART):
                unit(n)
            with act.Fori(0, LOOPS) as j:
                for n in range(HEADSTART, HEADSTART + UNITS):
                    unit(n, j)
            unit(N - 3)
            hid_round(N - 3)
            for n in range(N - 2, N):
                silu(n)
                hid_round(n)
            act.wait_ge(y_made, 3)
            act.dma_start(out_rows[:, 1, 2:T], y[:, 1, 2:T]).then_inc(out_stored[1], 16)
            act.wait_ge(out_stored[1], 32)

        @block.vector
        def _(dve):
            nc.vector.memset(blank[:], 0.0).then_inc(blank_made, 1)

            def statistics(b):
                dve.wait_ge(in_x[b], 16)
                for t in range(T):
                    nc.vector.bn_stats(stats[:, b * T + t], x_sb[:, b, t]).then_inc(stat1_step, 1)
                dve.wait_ge(stat1_step, 2 * T * b + T)
                for t in range(T):
                    nc.vector.bn_aggr(mean_var[:, b * T + t], stats[:, b * T + t]).then_inc(stat1_step, 1)
                dve.wait_ge(stat1_step, 2 * T * b + 2 * T)
                nc.vector.tensor_scalar(var_eps[:, b], mean_var[:, b * T:(b + 1) * T, 1], LN_EPS, None,
                                        ALU.add).then_inc(var1_made, 1)

            def exp_scale(b):
                dve.wait_ge(pow1, b + 1)
                nc.vector.tensor_scalar(rstd_scale[:, b * T:(b + 1) * T], rstd[:, b], SCALE, None,
                                        ALU.mult).then_inc(scale1_made, 1)

            dve.wait_ge(ctxT_made, 1)
            nc.vector.tensor_copy(ctxT[:], bank[7][:, 0:B * M]).then_inc(ctxT_out, 1)
            statistics(0)
            dve.wait_ge(k_zeroed, 1)
            dve.wait_ge(k_made, 1)
            for r in range(2):
                rows = slice(DH * r, DH * r + DH)
                nc.vector.tensor_copy(k_diag[rows, :, r],
                                      bank[5][rows, 0:HC * B * M].rearrange("p (c k) -> p c k", c=HC)).then_inc(k_out, 1)
            dve.wait_ge(tanh_made, 1)
            dve.wait_ge(in_bo, 16)
            nc.vector.tensor_scalar(bo_sb[:], bo_sb[:], g_tanh[:, 0:1], None, ALU.mult).then_inc(bo_scaled, 1)
            dve.wait_ge(rwT_made, 1)
            nc.vector.tensor_copy(rwT[:], bank[1][:, 0:E]).then_inc(rwT_out, 1)
            dve.wait_ge(rwT_out, 1)
            nc.vector.tensor_copy(rwT_parts[:, 0], rwT[:]).then_inc(rwT_out, 1)
            dve.wait_ge(rwT_out, 2)
            nc.vector.tensor_tensor(rwT_parts[:, 1], rwT[:], rwT_parts[:, 0].bitcast(F32),
                                    ALU.subtract).then_inc(rwT_out, 1)
            statistics(1)
            exp_scale(0)

            def shift(p):
                dve.wait_ge(scores_made, p + 1)
                sc = bank[p % 2][:].rearrange("p (h m) -> p h m", m=M)
                nc.vector.tensor_reduce(row_max[:, p % 2], sc, AX_X, ALU.max).then_inc(max_made, 1)
                dve.wait_ge(max_made, p + 1)
                if p >= 2:
                    dve.wait_ge(exp_made, 2 * p - 2)
                nc.vector.tensor_tensor(shifted[:, p % 2].rearrange("p t (h m) -> p (t h) m", m=M), sc,
                                        row_max[:, p % 2].unsqueeze(2).broadcast_to([P, 2 * HEADS, M]),
                                        ALU.subtract).then_inc(shift_made, 1)

            def sums(p):
                dve.wait_ge(exp_made, 2 * p + 2)
                nc.vector.tensor_reduce(row_sum[:, p % 2], expd[:, p % 2].rearrange("p t (h m) -> p (t h) m", m=M),
                                        AX_X, ALU.add).then_inc(sum_made, 1)
                dve.wait_ge(sum_made, p + 1)
                if p >= 2:
                    dve.wait_ge(probs_made[p - 2], 1)
                nc.vector.reciprocal(row_inv[:, p % 2], row_sum[:, p % 2]).then_inc(inv_made, 1)

            def add_attention(p):
                b, t = p // 2, 2 * (p % 2)
                dve.wait_ge(attn_made, p + 1)
                dve.wait_ge(bias_made, 1 + b)
                nc.vector.scalar_tensor_tensor(out=x2[:, b, t:t + 2], in0=attn_bank[p][:, 0:2 * D].rearrange("p (t d) -> p t d", t=2),
                                               scalar=g_tanh[:, 0:1], in1=x_bias[:, b, t:t + 2],
                                               op0=ALU.mult, op1=ALU.add).then_inc(x2_made, 1)

            def moments(p):
                b, t = p // 2, 2 * (p % 2)
                dve.wait_ge(x2_made, p + 1)
                for i in range(2):
                    nc.vector.bn_stats(stats2[:, 2 * p + i], x2[:, b, t + i]).then_inc(stat2_step, 1)

            def aggregate(p):
                dve.wait_ge(stat2_step, 4 * p + 2)
                for i in range(2):
                    nc.vector.bn_aggr(mean_var2[:, 2 * p + i], stats2[:, 2 * p + i]).then_inc(stat2_step, 1)

            def residual(p):
                add_attention(p)
                moments(p)
                aggregate(p)

            def statistics2(b):
                dve.wait_ge(stat2_step, 8 * b + 8)
                nc.vector.tensor_scalar(var_eps2[:, b], mean_var2[:, b * T:(b + 1) * T, 1], LN_EPS, None,
                                        ALU.add).then_inc(ln2, 1)

            def normalise2(b):
                dve.wait_ge(pow2, b + 1)
                for t in range(T):
                    nc.vector.tensor_scalar(xn2[:, b * T + t], x2[:, b, t], mean_var2[:, b * T + t, 0:1],
                                            rstd2[:, b, t:t + 1], ALU.subtract, ALU.mult).then_inc(xn2_made, 1)

            def tokens2_rest(b):
                dve.wait_ge(xn2_hi_made, b + 1)
                nc.vector.tensor_tensor(xn2T_lo[:, b], bank[6][:], xn2T_hi[:, b].bitcast(F32),
                                        ALU.subtract).then_inc(xn2_lo_made, 1)

            def sum_logits(b):
                dve.wait_ge(logits_made, b + 1)
                nc.vector.tensor_reduce(logits[:, b * T:(b + 1) * T],
                                        logits_bank[b][:, 0:T * 2 * E].rearrange("p (t w e) -> p t e w", w=2, e=E),
                                        AX_X, ALU.add).then_inc(logits_out, 1)

            def top_values(b):
                dve.wait_ge(logits_out, b + 1)
                for t in range(T):
                    top = nc.vector.max(top8[:, b * T + t], logits[:, b * T + t])
                top.then_inc(top8_made, 1)

            def top_places(b):
                dve.wait_ge(top8_made, b + 1)
                for t in range(T):
                    at = nc.vector.max_index(top8_at[:, b * T + t], top8[:, b * T + t], logits[:, b * T + t])
                at.then_inc(top8_at_made, 1)

            def mark_chosen(b):
                dve.wait_ge(const_made, 3)
                dve.wait_ge(top8_at_made, b + 1)
                nc.vector.tensor_tensor(is_chosen[:, b].rearrange("p (t k) e -> p t k e", k=2),
                                        expert_no[:].unsqueeze(1).unsqueeze(1).broadcast_to([P, T, 2, E]),
                                        top8_at[:, b * T:(b + 1) * T, 0:2].unsqueeze(3).broadcast_to([P, T, 2, E]),
                                        ALU.is_equal).then_inc(chosen_made, 1)

            def gate_values(b):
                pair = "p (t k) -> p t k"
                sig = top2_sig[:, b, 0].rearrange(pair, k=2)
                dve.wait_ge(gate_exp_made, b + 1)
                nc.vector.tensor_scalar(top2_exp[:, b, 1], top2_exp[:, b, 0], 1.0, None, ALU.add).then_inc(gate_step, 1)
                yield
                dve.wait_ge(gate_step, 6 * b + 1)
                nc.vector.reciprocal(top2_sig[:, b, 0], top2_exp[:, b, 1]).then_inc(gate_step, 1)
                yield
                dve.wait_ge(gate_step, 6 * b + 2)
                nc.vector.scalar_tensor_tensor(out=gate_sum[:, b, 0], in0=sig[:, :, 0], scalar=GATE_EPS,
                                               in1=sig[:, :, 1], op0=ALU.add, op1=ALU.add).then_inc(gate_step, 1)
                yield
                dve.wait_ge(gate_step, 6 * b + 3)
                nc.vector.reciprocal(gate_sum[:, b, 1], gate_sum[:, b, 0]).then_inc(gate_step, 1)
                yield
                dve.wait_ge(gate_step, 6 * b + 4)
                nc.vector.tensor_tensor(top2_sig[:, b, 1].rearrange(pair, k=2), sig,
                                        gate_sum[:, b, 1].unsqueeze(2).broadcast_to([P, T, 2]), ALU.mult).then_inc(gate_step, 1)
                yield
                dve.wait_ge(gate_step, 6 * b + 5)
                dve.wait_ge(chosen_made, b + 1)
                nc.vector.tensor_tensor(chosen_gate[:, b], is_chosen[:, b],
                                        top2_sig[:, b, 1].unsqueeze(2).broadcast_to([P, 2 * T, E]), ALU.mult).then_inc(gate_step, 1)
                yield
                dve.wait_ge(gate_step, 6 * b + 6)
                both = chosen_gate[:, b].rearrange("p (t k) e -> p t k e", k=2)
                nc.vector.tensor_tensor(gates[:, b * T:(b + 1) * T], both[:, :, 0], both[:, :, 1], ALU.add).then_inc(gates_made, 1)
                yield

            def gatesT_copy(b):
                dve.wait_ge(gatesT_made, b + 1)
                nc.vector.tensor_copy(gatesT[:, b * S:(b + 1) * S], gatesT_bank[0:E, :]).then_inc(gatesT_out, 1)

            def hidden(n, first=0):
                dve.wait_ge(silu_done, first + (n + 1))
                dve.wait_ge(up_done, first + (n + 1))
                if n >= 2:
                    dve.wait_ge(hid_lo_done, first + (n - 1))
                nc.vector.tensor_tensor(hid[:, n % 2], up_bank[n % 2][:], silu_g[:, n % 2], ALU.mult).then_inc(hid_done, 1)

            def hidden_rest(n, first=0):
                dve.wait_ge(hid_hi_done, first + (n + 1))
                nc.vector.tensor_tensor(hid_lo[:, n % 4], hid[:, n % 2], hid_hi[:, n % 4].bitcast(F32),
                                        ALU.subtract).then_inc(hid_lo_done, 1)

            def weigh(q, j=0, part=None):
                cols = slice(0, S) if part is None else slice(part * S // 2, (part + 1) * S // 2)
                dve.wait_ge(down_done, j * UNITS + (2 * q + 2))
                if q < PAIRS:
                    dve.wait_ge(gate_spread, q + 1)
                else:
                    dve.wait_ge(in_gate_row[q % PAIRS], (j + q // PAIRS) * 16)
                dve.wait_ge(acc_done, j * PAIRS + (q + 1))
                nc.vector.tensor_tensor(weighted[:, q % 2, cols], down_bank[q % 2][:, cols],
                                        gate_row[:, q % PAIRS, cols], ALU.mult).then_inc(weighted_done, 1)

            def unit(n, j=0):
                hidden(n, j * UNITS)
                if n > RESTS_BEHIND:
                    hidden_rest(n - 1, j * UNITS)
                if n % 2 == 0:
                    weigh((n - 4) // 2, j)

            shift(0)
            shift(1)
            sums(0)
            normalise(dve, 0)
            sums(1)
            normalise(dve, 1)
            exp_scale(1)
            shift(2)
            add_attention(0)
            moments(0)
            add_attention(1)
            aggregate(0)
            moments(1)
            aggregate(1)
            statistics2(0)
            sums(2)
            normalise2(0)
            shift(3)
            tokens2_rest(0)
            sums(3)
            residual(2)

            first_gates = gate_values(0)
            second_gates = gate_values(1)
            hidden(0)
            sum_logits(0)
            top_values(0)
            hidden_rest(0)
            hidden(1)
            residual(3)
            statistics2(1)
            hidden_rest(1)
            hidden(2)
            normalise2(1)
            hidden_rest(2)
            hidden(3)
            tokens2_rest(1)
            hidden_rest(3)
            top_places(0)
            mark_chosen(0)
            for _ in range(7):
                next(first_gates)
            hidden(4)
            hidden_rest(4)
            hidden(5)
            weigh(0)
            sum_logits(1)
            top_values(1)
            top_places(1)
            hidden_rest(5)
            mark_chosen(1)
            hidden(6)
            next(second_gates)
            next(second_gates)
            weigh(1)
            hidden_rest(6)
            next(second_gates)
            next(second_gates)
            next(second_gates)
            hidden(7)
            next(second_gates)
            next(second_gates)
            gatesT_copy(0)
            hidden_rest(7)
            hidden(8)
            hidden_rest(8)
            hidden(9)
            weigh(2)
            hidden_rest(9)
            gatesT_copy(1)
            hidden(10)
            weigh(3)
            hidden_rest(10)
            for n in range(RESTS_BEHIND, HEADSTART):
                unit(n)
            with dve.Fori(0, LOOPS) as j:
                for n in range(HEADSTART, HEADSTART + UNITS):
                    unit(n, j)
            unit(N - 3)
            hidden_rest(N - 3)
            hidden(N - 2)
            weigh(Q - 3)
            hidden_rest(N - 2)
            hidden(N - 1)
            weigh(Q - 2)
            hidden_rest(N - 1)

            def result(b, tiles, i):
                dve.wait_ge(accT_made, i + 1)
                nc.vector.scalar_tensor_tensor(
                    out=y[:, b, tiles], in0=sum_bank[i][:].rearrange("p (t d) -> p t d", t=T)[:, 0:tiles.stop - tiles.start],
                    scalar=g_tanh[:, 1:2], in1=x2[:, b, tiles], op0=ALU.mult, op1=ALU.add).then_inc(y_made, 1)

            result(0, slice(0, T), 0)
            for i in range(2):
                weigh(Q - 1, part=i)
            for i in range(2):
                result(1, slice(2 * i, 2 * i + 2), i + 1)

        @block.tensor
        def _(pe):
            def keep_warm(times, free_bank):
                for _ in range(times):
                    nc.tensor.matmul(free_bank[:].rearrange("p (r n) -> p r n", n=P), blank[:],
                                     blank[:].unsqueeze(1).broadcast_to([P, 4, P]), start=True, stop=True)

            pe.wait_ge(blank_made, 1)
            keep_warm(WARM_INPUTS, bank[0])
            pe.wait_ge(ident_made, 1)
            pe.wait_ge(in_ctx, 16)
            nc.tensor.transpose(bank[7][:, 0:B * M], ctx_sb[:], ident[0:B * M, 0:B * M]).then_inc(ctxT_made, 1)

            def project_ctx(w, w_in, bk, made):
                pe.wait_ge(w_in, 16)
                for c in range(HC):
                    mm = nc.tensor.matmul(bk[:, c * B * M:(c + 1) * B * M], w[:, c * P:(c + 1) * P], ctxT[:],
                                          start=True, stop=True)
                mm.then_inc(made, 1)

            def turn_tokens(b):
                pe.wait_ge(in_x[b], 16)
                for t in range(T):
                    mm = nc.tensor.transpose(bank[2 + b][:, t * P:(t + 1) * P], x_sb[:, b, t], ident[:])
                mm.then_inc(xT_made, 1)

            keep_warm(WARM_CTX, bank[0])
            pe.wait_ge(ctxT_out, 1)
            project_ctx(wk_sb, in_wk, bank[5], k_made)
            pe.wait_ge(center_made, 1)
            pe.wait_ge(in_wq, 16)
            for c in range(HC):
                mm = nc.tensor.matmul(bank[6][:, c * D:(c + 1) * D], wq_sb[:, c * P:(c + 1) * P], center[:],
                                      start=True, stop=True)
            mm.then_inc(wqT_made, 1)
            turn_tokens(0)
            pe.wait_ge(in_rw, 16)
            nc.tensor.transpose(bank[1][:, 0:E], rw_sb[:], ident[0:E, 0:E]).then_inc(rwT_made, 1)
            pe.wait_ge(wqT_out, 1)
            pe.wait_ge(k_out, 2)
            for c in range(HC):
                mm = nc.tensor.matmul(bank[4][:, c * P:(c + 1) * P], wqT[:, c], k_diag[:, c].rearrange("p r k -> p (r k)"),
                                      start=True, stop=True)
            mm.then_inc(m_made, 1)
            turn_tokens(1)

            def fold_out():
                pe.wait_ge(v_out, 4)
                pe.wait_ge(in_wo, 16)
                for b in range(B):
                    for g in range(2):
                        for k in range(2):
                            mm = nc.tensor.matmul(bank[5][:, (2 * b + g) * D:(2 * b + g + 1) * D], v_diag[:, b, g, k],
                                                  wo_sb[:, 2 * g + k], start=(k == 0), stop=(k == 1))
                mm.then_inc(u_made, 1)

            def scores(p):
                b = p // 2
                pe.wait_ge(xT_out, b + 1)
                pe.wait_ge(m_out, 1)
                if p >= 2:
                    pe.wait_ge(shift_made, p - 1)
                for t in range(2):
                    mm = nc.tensor.matmul(bank[p % 2][:, t * HM:(t + 1) * HM], xT[:, 2 * p + t],
                                          m_sb[:, b].rearrange("p h m -> p (h m)"), start=True, stop=True)
                mm.then_inc(scores_made, 1)

            def turn_probs(p):
                pe.wait_ge(probs_made[p], 1)
                if p < 2:
                    pe.wait_ge(xT_out, p + 1)
                else:
                    pe.wait_ge(x2_made, 2)
                for t in range(2):
                    for g in range(2):
                        at = (2 * t + g) * P
                        mm = nc.tensor.transpose(probsT_bank[p][:, at:at + P], probs[:, p % 2, t, g * P:(g + 1) * P], ident[:])
                mm.then_inc(probsT_made, 1)

            def attention(p):
                b = p // 2
                pe.wait_ge(probsT_out, p + 1)
                pe.wait_ge(u_out, 1)
                for t in range(2):
                    for g in range(2):
                        mm = nc.tensor.matmul(attn_bank[p][:, t * D:(t + 1) * D], probsT[:, p % 2, t, g],
                                              u_sb[:, b, g], start=(g == 0), stop=(g == 1))
                mm.then_inc(attn_made, 1)

            def turn_tokens2(b):
                for t in range(T):
                    pe.wait_ge(xn2_made, T * b + t + 1)
                    mm = nc.tensor.transpose(bank[6][:, t * P:(t + 1) * P], xn2[:, b * T + t], ident[:])
                mm.then_inc(xn2T_made, 1)

            def route(b):
                pe.wait_ge(rwT_out, 3)
                pe.wait_ge(xn2_lo_made, b + 1)
                if b == 1:
                    pe.wait_ge(x2_made, 4)
                for t in range(T):
                    for i, xt in enumerate((xn2T_hi, xn2T_lo)):
                        mm = nc.tensor.matmul(logits_bank[b][:, t * 2 * E:(t + 1) * 2 * E], xt[:, b, t * P:(t + 1) * P],
                                              rwT_parts[:].rearrange("p w e -> p (w e)"), start=(i == 0), stop=(i == 1))
                mm.then_inc(logits_made, 1)

            def spread_gates(b, k):
                pe.wait_ge(gates_made, b + 1)
                if (b, k) != (0, 0):
                    pe.wait_ge(gate_spread, b * EP + k)
                for t in range(T):
                    mm = nc.tensor.transpose(spread_bank[:, t * P:(t + 1) * P],
                                             gates[:, b * T + t, k:k + 1].broadcast_to([P, P]), ident[:])
                mm.then_inc(spread_made, 1)

            def turn_gates(b):
                pe.wait_ge(gates_made, b + 1)
                if b == 0:
                    pe.wait_ge(logits_out, 2)
                else:
                    pe.wait_ge(gatesT_out, 1)
                for t in range(T):
                    mm = nc.tensor.transpose(gatesT_bank[0:E, t * P:(t + 1) * P], gates[:, b * T + t], ident[:])
                mm.then_inc(gatesT_made, 1)

            scores(0)
            pe.wait_ge(rwT_out, 1)
            scores(1)
            project_ctx(wv_sb, in_wv, bank[7], v_made)
            scores(2)
            fold_out()
            turn_probs(0)
            scores(3)
            turn_probs(1)
            attention(0)
            attention(1)
            keep_warm(WARM_NORM, bank[6])
            turn_tokens2(0)
            turn_probs(2)

            def gate_up(n, j=0, first_of_half=False):
                half, k, c = unit_of(n)
                cols = slice(c * P, (c + 1) * P)
                dest = ((gate_bank[n % 2], gate_done), (up_bank[n % 2], up_done))

                def product(i, w, xt, start=False, stop=False):
                    mm = nc.tensor.matmul(dest[i][0][:], w[:, k, i, cols], xt[:, half], start=start, stop=stop)
                    if stop:
                        mm.then_inc(dest[i][1], 1)

                pe.wait_ge(w_lo_done, (j + n // UNITS) * 4 + (k + 1))
                if n >= 2:
                    pe.wait_ge(hid_done, j * UNITS + (n - 1))
                if first_of_half:
                    pe.wait_ge(xn2_hi_made, half + 1)
                    for i in range(2):
                        product(i, gu_hi, xn2T_hi, start=True)
                        product(i, gu_lo, xn2T_hi)
                    pe.wait_ge(xn2_lo_made, half + 1)
                    for i in range(2):
                        product(i, gu_hi, xn2T_lo, stop=True)
                else:
                    for i in range(2):
                        product(i, gu_hi, xn2T_hi, start=True)
                        product(i, gu_lo, xn2T_hi)
                        product(i, gu_hi, xn2T_lo, stop=True)

            def down(n, j=0, rest_apart=False):
                half, k, c = unit_of(n)
                q = n // FC
                if rest_apart:
                    pe.wait_ge(hid_hi_done, j * UNITS + (n + 1))
                else:
                    pe.wait_ge(hid_lo_done, j * UNITS + (n + 1))
                pe.wait_ge(w_lo_done, (j + n // UNITS) * 4 + (k + 3))
                if c == 0 and q >= 2:
                    pe.wait_ge(weighted_done, j * PAIRS + (q - 1))
                terms = [(d_hi, hid_hi), (d_lo, hid_hi), (d_hi, hid_lo)]
                for s, (w, h) in enumerate(terms):
                    if rest_apart and h is hid_lo:
                        pe.wait_ge(hid_lo_done, j * UNITS + (n + 1))
                    mm = nc.tensor.matmul(down_bank[q % 2][:], w[:, k, c], h[:, n % 4],
                                          start=(c == 0 and s == 0), stop=(c == FC - 1 and s == len(terms) - 1))
                mm.then_inc(down_done, 1)

            pe.wait_ge(shift_made, 3)
            pe.wait_ge(probsT_out, 2)
            gate_up(0, first_of_half=True)
            attention(2)
            route(0)
            turn_probs(3)
            pe.wait_ge(shift_made, 4)
            gate_up(1)
            attention(3)
            gate_up(2)
            down(0)
            gate_up(3)
            down(1)
            pe.wait_ge(logits_out, 1)
            turn_tokens2(1)
            down(2)
            gate_up(4, first_of_half=True)
            route(1)
            gate_up(5)
            down(3)
            spread_gates(0, 0)
            for n in range(6, HEADSTART):
                gate_up(n)
                if n in SPREAD_AT:
                    q = SPREAD_AT.index(n)
                    spread_gates(q // EP, q % EP)
                down(n - LAG)
                if n in TURN_AT:
                    turn_gates(TURN_AT.index(n))
            with pe.Fori(0, LOOPS) as j:
                for n in range(HEADSTART, HEADSTART + UNITS):
                    gate_up(n, j)
                    down(n - LAG, j)
            for n in range(N - 3, N):
                gate_up(n)
                down(n - LAG)

            def turn_sum(bk, parts, start, stop):
                width = parts[0].shape[-1]
                for i, part in enumerate(parts):
                    for t in range(width // P):
                        mm = nc.tensor.matmul(bk[:, t * P:(t + 1) * P], part[:, t * P:(t + 1) * P], ident[:],
                                              start=(start and i == 0 and t == 0),
                                              stop=(stop and i == len(parts) - 1 and t == width // P - 1))
                return mm

            halves = [slice(0, S // 2), slice(S // 2, S)]
            pe.wait_ge(acc_done, B + Q - 4)
            pe.wait_ge(hid_done, N - 1)
            for i in range(2):
                turn_sum(sum_bank[1 + i], [acc[:, 1, halves[i]]], True, False)
            down(N - 2)
            pe.wait_ge(acc_done, B + Q - 2)
            for t in range(T):
                mm = nc.tensor.transpose(sum_bank[0][:, t * P:(t + 1) * P], acc[:, 0, t * P:(t + 1) * P], ident[:])
            mm.then_inc(accT_made, 1)
            pe.wait_ge(weighted_done, Q - 1)
            turn_sum(sum_bank[1], [weighted[:, (Q - 2) % 2, halves[0]]], False, False)
            down(N - 1, rest_apart=True)
            turn_sum(sum_bank[2], [weighted[:, (Q - 2) % 2, halves[1]]], False, False)
            for i in range(2):
                pe.wait_ge(weighted_done, Q + i)
                turn_sum(sum_bank[1 + i], [weighted[:, (Q - 1) % 2, halves[i]]], False, True).then_inc(accT_made, 1)


_INS = ['x', 'ctx_1024', 'g_xattn', 'g_ffn', 'L0_xattn_Wq', 'L0_xattn_Wk', 'L0_xattn_Wv', 'L0_xattn_Wo',
        'L0_xattn_bo', 'L0_ffn_router_w', 'L0_ffn_w_gate', 'L0_ffn_w_up', 'L0_ffn_w_down']
_OUTS = [((2, 512, 128), 'float32')]


def kernel(**inputs):
    import numpy as _np
    import concourse.bacc as _bacc
    from concourse import mybir as _mybir
    from concourse.bass_utils import run_bass_kernel_spmd as _run

    nc = _bacc.Bacc("TRN2", target_bir_lowering=False, num_devices=1)
    arrays, args = {}, []
    for name in _INS:
        a = _np.ascontiguousarray(inputs[name])
        arrays[f"in_{name}_dram"] = a
        args.append(nc.dram_tensor(f"in_{name}_dram", a.shape, _mybir.dt.from_np(a.dtype), kind="ExternalInput").ap())
    for i, (shape, dtype) in enumerate(_OUTS):
        dt = _mybir.dt.from_np(_np.dtype(dtype))
        args.append(nc.dram_tensor(f"out_{i}_dram", shape, dt, kind="ExternalOutput").ap())
    gated_cross_attention_and_top2_experts(nc, *args)
    r = _run(nc, [arrays], core_ids=[0])
    got = tuple(r.results[0][f"out_{i}_dram"] for i in range(len(_OUTS)))
    return got[0]
```
